# Optimizing a Trainium2 kernel written in Bass

```python
import numpy as np
import jax
import jax.numpy as jnp

def _softmax(x, axis=-1):
    return jax.nn.softmax(x, axis=axis)

def _gelu(x):
    return jax.nn.gelu(x, approximate=True)

def _silu(x):
    return jax.nn.silu(x)

def _sigmoid(x):
    return jax.nn.sigmoid(x)

def _layernorm(x, axis=-1, eps=1e-05):
    m = jnp.mean(x, axis=axis, keepdims=True)
    v = jnp.var(x, axis=axis, keepdims=True)
    return (x - m) / jnp.sqrt(v + eps)

def _scatter_add(tgt, idx, src, axis=0):
    return tgt.at[idx].add(src)

def _segment_sum(src, seg, n):
    return jax.ops.segment_sum(src, seg, n)
kernel_name = 'mk_gnn_resnorm_d4_gnn_r16_52c12a'

def setup_inputs(seed: int=0):
    np.random.seed(seed)
    _w = jnp.asarray

    def _rec_inputs():
        import jax
        import jax.numpy as jnp
        _gk = jax.random.key(seed)
        x = -0.0009044 + 1 * jax.random.normal(jax.random.fold_in(_gk, 1), (6250, 32), jnp.float32)
        src = jax.random.randint(jax.random.fold_in(_gk, 2), (200000,), 0, 6250, jnp.int32)
        dst = jax.random.randint(jax.random.fold_in(_gk, 3), (200000,), 0, 6250, jnp.int32)
        _o = jnp.argsort(dst, stable=True)
        src = src[_o]
        dst = dst[_o]
        edge_attr_16 = 0.000196303 + 1.00016 * jax.random.normal(jax.random.fold_in(_gk, 12), (200000, 16), jnp.float32)
        edge_attr_2 = jax.random.uniform(jax.random.fold_in(_gk, 13), (200000, 2), jnp.float32, 0.0, 1)
        edge_attr_32 = -9.77346e-05 + 0.999888 * jax.random.normal(jax.random.fold_in(_gk, 14), (200000, 32), jnp.float32)
        return (x, src, dst, edge_attr_16, edge_attr_2, edge_attr_32)
    x, src, dst, edge_attr_16, edge_attr_2, edge_attr_32 = _rec_inputs()

    def _L0_gnn_setup():
        import jax, jax.numpy as jnp
        import numpy as np
        N_NODES = 3125
        N_EDGES = 100000
        D_FEAT = 32
        key = jax.random.key(seed)
        k1, k2, k3, k4 = jax.random.split(key, 4)
        node_feat = jax.random.normal(k1, (N_NODES, D_FEAT), dtype=jnp.float32)
        edge_feat = jax.random.normal(k2, (N_EDGES, D_FEAT), dtype=jnp.float32)
        eps = jnp.zeros((1,), dtype=jnp.float32)
        src = jax.random.randint(k3, (N_EDGES,), 0, N_NODES, dtype=jnp.int64)
        dst = jax.random.randint(k4, (N_EDGES,), 0, N_NODES, dtype=jnp.int64)
        return {'node_feat': node_feat, 'edge_feat': edge_feat, 'eps': eps, 'src': src, 'dst': dst}
    _L0_gnn_all = _L0_gnn_setup()
    _L0_gnn_in = {k: v for k, v in _L0_gnn_all.items() if k in ('eps',)}
    del _L0_gnn_all

    def _L1_gnn_setup():
        import jax, jax.numpy as jnp
        import numpy as np
        N_NODES = 6250
        N_EDGES = 100000
        D_FEAT = 32
        EPS = 1e-12
        key = jax.random.key(seed)
        k1, k2, k3 = jax.random.split(key, 3)
        feat = jax.random.normal(k1, (N_NODES, D_FEAT), dtype=jnp.float32)
        beta = jnp.ones((1,), dtype=jnp.float32)
        src = jax.random.randint(k2, (N_EDGES,), 0, N_NODES, dtype=jnp.int32)
        dst = jax.random.randint(k3, (N_EDGES,), 0, N_NODES, dtype=jnp.int32)
        return {'feat': feat, 'beta': beta, 'src': src, 'dst': dst}
    _L1_gnn_all = _L1_gnn_setup()
    _L1_gnn_in = {k: v for k, v in _L1_gnn_all.items() if k in ('beta',)}
    del _L1_gnn_all

    def _L2_gnn_setup():
        import jax, jax.numpy as jnp
        import numpy as np
        import itertools
        N = 6250
        E = 100000
        DIM = 2
        K = 5
        K_TOT = K ** DIM
        IS_OPEN = True
        M_IN = 32
        M_OUT = 32
        S = 2 ** DIM

        def spline_basis_deg1(pseudo):
            scale = K - 1 if IS_OPEN else K
            p = pseudo * scale
            lo_f = jnp.floor(p)
            frac = p - lo_f
            lo = lo_f.astype(jnp.int32)
            strides = [K ** d for d in range(DIM)]
            bases, idxs = ([], [])
            for s in itertools.product((0, 1), repeat=DIM):
                b = jnp.ones(p.shape[0], p.dtype)
                flat = jnp.zeros(p.shape[0], jnp.int32)
                for d, sd in enumerate(s):
                    b = b * (frac[:, d] if sd else 1.0 - frac[:, d])
                    i = lo[:, d] + sd
                    i = jnp.clip(i, 0, K - 1) if IS_OPEN else jnp.mod(i, K)
                    flat = flat + i * strides[d]
                bases.append(b)
                idxs.append(flat)
            return (jnp.stack(bases, axis=1), jnp.stack(idxs, axis=1))
        key = jax.random.key(seed)
        k1, k2, k3, k4, k5, k6 = jax.random.split(key, 6)
        x = jax.random.normal(k1, (N, M_IN), dtype=jnp.float32)
        edge_index = jax.random.randint(k2, (2, E), 0, N, dtype=jnp.int64)
        pseudo = jax.random.uniform(k3, (E, DIM), dtype=jnp.float32)
        bound = 1.0 / np.sqrt(M_IN * K_TOT)
        weight = jax.random.uniform(k4, (K_TOT, M_IN, M_OUT), jnp.float32, -bound, bound)
        root_weight = jax.random.uniform(k5, (M_IN, M_OUT), jnp.float32, -bound, bound)
        bias = jax.random.uniform(k6, (M_OUT,), jnp.float32, -bound, bound)
        return {'x': x, 'edge_index': edge_index, 'pseudo': pseudo, 'weight': weight, 'root_weight': root_weight, 'bias': bias}
    _L2_gnn_all = _L2_gnn_setup()
    _L2_gnn_in = {k: v for k, v in _L2_gnn_all.items() if k in ('weight', 'root_weight', 'bias')}
    del _L2_gnn_all

    def _L3_gnn_setup():
        import jax, jax.numpy as jnp
        import numpy as np
        N = 3125
        E = 100000
        F = 32
        T = 4
        FT = F // T
        ED = 16
        L = 5

        def _pna_layer(x, src, dst, edge_attr, eW, eb, pW, pb, poW, pob, lW, lb):
            n = x.shape[0]
            xt = x.reshape(n, T, FT)
            ee = edge_attr @ eW + eb
            xi = xt[dst]
            xj = xt[src]
            ee_b = jnp.broadcast_to(ee[:, None, :], (ee.shape[0], T, FT))
            h = jnp.concatenate([xi, xj, ee_b], axis=-1)
            h = jnp.einsum('etk,tkf->etf', h, pW) + pb
            ssum = jax.ops.segment_sum(h, dst, num_segments=n)
            cnt = jax.ops.segment_sum(jnp.ones((h.shape[0],), h.dtype), dst, num_segments=n)
            mean = ssum / jnp.maximum(cnt, 1.0)[:, None, None]
            mx = jax.ops.segment_max(h, dst, num_segments=n)
            mx = jnp.where(cnt[:, None, None] > 0, mx, 0.0)
            out = jnp.concatenate([xt, mean, ssum, mx], axis=-1)
            out = jnp.einsum('ntk,tkf->ntf', out, poW) + pob
            out = out.reshape(n, T * FT) @ lW + lb
            return jax.nn.relu(out)
        key = jax.random.key(seed)
        ks = jax.random.split(key, 11)
        s = 0.2
        return {'x': jax.random.normal(ks[0], (N, F), jnp.float32), 'edge_index': jax.random.randint(ks[1], (2, E), 0, N, dtype=jnp.int32), 'edge_attr': jax.random.normal(ks[2], (E, ED), jnp.float32), 'edge_W': jax.random.normal(ks[3], (L, ED, FT), jnp.float32) * s, 'edge_b': jax.random.normal(ks[4], (L, FT), jnp.float32) * s, 'pre_W': jax.random.normal(ks[5], (L, T, 3 * FT, FT), jnp.float32) * s, 'pre_b': jax.random.normal(ks[6], (L, T, FT), jnp.float32) * s, 'post_W': jax.random.normal(ks[7], (L, T, 4 * FT, FT), jnp.float32) * s, 'post_b': jax.random.normal(ks[8], (L, T, FT), jnp.float32) * s, 'lin_W': jax.random.normal(ks[9], (L, T * FT, F), jnp.float32) * s, 'lin_b': jax.random.normal(ks[10], (L, F), jnp.float32) * s}
    _L3_gnn_all = _L3_gnn_setup()
    _L3_gnn_in = {k: v for k, v in _L3_gnn_all.items() if k in ('edge_W', 'edge_b', 'pre_W', 'pre_b', 'post_W', 'post_b', 'lin_W', 'lin_b')}
    del _L3_gnn_all
    return {'x': x, 'src': src, 'dst': dst, 'edge_attr_16': edge_attr_16, 'edge_attr_2': edge_attr_2, 'edge_attr_32': edge_attr_32, 'L0_gnn_eps': _L0_gnn_in['eps'], 'L1_gnn_beta': _L1_gnn_in['beta'], 'L2_gnn_weight': _L2_gnn_in['weight'], 'L2_gnn_root_weight': _L2_gnn_in['root_weight'], 'L2_gnn_bias': _L2_gnn_in['bias'], 'L3_gnn_edge_W': _L3_gnn_in['edge_W'], 'L3_gnn_edge_b': _L3_gnn_in['edge_b'], 'L3_gnn_pre_W': _L3_gnn_in['pre_W'], 'L3_gnn_pre_b': _L3_gnn_in['pre_b'], 'L3_gnn_post_W': _L3_gnn_in['post_W'], 'L3_gnn_post_b': _L3_gnn_in['post_b'], 'L3_gnn_lin_W': _L3_gnn_in['lin_W'], 'L3_gnn_lin_b': _L3_gnn_in['lin_b']}

def reference(x, src, dst, edge_attr_16, edge_attr_2, edge_attr_32, L0_gnn_eps, L1_gnn_beta, L2_gnn_weight, L2_gnn_root_weight, L2_gnn_bias, L3_gnn_edge_W, L3_gnn_edge_b, L3_gnn_pre_W, L3_gnn_pre_b, L3_gnn_post_W, L3_gnn_post_b, L3_gnn_lin_W, L3_gnn_lin_b):
    import jax
    import jax.numpy as jnp

    def _L0_gnn_ref(node_feat, edge_feat, eps, src, dst):
        import jax, jax.numpy as jnp
        import numpy as np
        N_NODES = 3125
        N_EDGES = 100000
        D_FEAT = 32
        m = jax.nn.relu(node_feat[src] + edge_feat)
        neigh = jax.ops.segment_sum(m, dst, num_segments=node_feat.shape[0])
        return (1.0 + eps[0]) * node_feat + neigh

    def _L1_gnn_ref(feat, beta, src, dst):
        import jax, jax.numpy as jnp
        import numpy as np
        N_NODES = 6250
        N_EDGES = 100000
        D_FEAT = 32
        EPS = 1e-12
        N = feat.shape[0]
        norm = jnp.maximum(jnp.linalg.norm(feat, axis=-1, keepdims=True), EPS)
        norm_h = feat / norm
        cos = jnp.sum(norm_h[src] * norm_h[dst], axis=-1)
        e = beta[0] * cos
        m = jax.lax.stop_gradient(jax.ops.segment_max(e, dst, num_segments=N))
        m = jnp.where(jnp.isfinite(m), m, 0.0)
        p = jnp.exp(e - m[dst])
        s = jax.ops.segment_sum(p, dst, num_segments=N)
        p = p / s[dst]
        out = jax.ops.segment_sum(feat[src] * p[:, None], dst, num_segments=N)
        return out

    def _L2_gnn_ref(x, edge_index, pseudo, weight, root_weight, bias):
        import jax, jax.numpy as jnp
        import numpy as np
        import itertools
        N = 6250
        E = 100000
        DIM = 2
        K = 5
        K_TOT = K ** DIM
        IS_OPEN = True
        M_IN = 32
        M_OUT = 32
        S = 2 ** DIM

        def spline_basis_deg1(pseudo):
            scale = K - 1 if IS_OPEN else K
            p = pseudo * scale
            lo_f = jnp.floor(p)
            frac = p - lo_f
            lo = lo_f.astype(jnp.int32)
            strides = [K ** d for d in range(DIM)]
            bases, idxs = ([], [])
            for s in itertools.product((0, 1), repeat=DIM):
                b = jnp.ones(p.shape[0], p.dtype)
                flat = jnp.zeros(p.shape[0], jnp.int32)
                for d, sd in enumerate(s):
                    b = b * (frac[:, d] if sd else 1.0 - frac[:, d])
                    i = lo[:, d] + sd
                    i = jnp.clip(i, 0, K - 1) if IS_OPEN else jnp.mod(i, K)
                    flat = flat + i * strides[d]
                bases.append(b)
                idxs.append(flat)
            return (jnp.stack(bases, axis=1), jnp.stack(idxs, axis=1))
        n = x.shape[0]
        row, col = (edge_index[0], edge_index[1])
        basis, idx = spline_basis_deg1(pseudo)
        x_j = x[col]
        h = jnp.zeros((n * K_TOT, x.shape[1]), dtype=x.dtype)
        for s in range(S):
            keys = row * K_TOT + idx[:, s]
            h = h + jax.ops.segment_sum(basis[:, s, None] * x_j, keys, num_segments=n * K_TOT)
        h = h.reshape(n, K_TOT, x.shape[1])
        out = jnp.einsum('nki,kio->no', h, weight)
        deg = jax.ops.segment_sum(jnp.ones(row.shape[0], x.dtype), row, num_segments=n)
        out = out / jnp.clip(deg, 1.0)[:, None]
        out = out + x @ root_weight + bias
        return out

    def _L3_gnn_ref(x, edge_index, edge_attr, edge_W, edge_b, pre_W, pre_b, post_W, post_b, lin_W, lin_b):
        import jax, jax.numpy as jnp
        import numpy as np
        N = 3125
        E = 100000
        F = 32
        T = 4
        FT = F // T
        ED = 16
        L = 5

        def _pna_layer(x, src, dst, edge_attr, eW, eb, pW, pb, poW, pob, lW, lb):
            n = x.shape[0]
            xt = x.reshape(n, T, FT)
            ee = edge_attr @ eW + eb
            xi = xt[dst]
            xj = xt[src]
            ee_b = jnp.broadcast_to(ee[:, None, :], (ee.shape[0], T, FT))
            h = jnp.concatenate([xi, xj, ee_b], axis=-1)
            h = jnp.einsum('etk,tkf->etf', h, pW) + pb
            ssum = jax.ops.segment_sum(h, dst, num_segments=n)
            cnt = jax.ops.segment_sum(jnp.ones((h.shape[0],), h.dtype), dst, num_segments=n)
            mean = ssum / jnp.maximum(cnt, 1.0)[:, None, None]
            mx = jax.ops.segment_max(h, dst, num_segments=n)
            mx = jnp.where(cnt[:, None, None] > 0, mx, 0.0)
            out = jnp.concatenate([xt, mean, ssum, mx], axis=-1)
            out = jnp.einsum('ntk,tkf->ntf', out, poW) + pob
            out = out.reshape(n, T * FT) @ lW + lb
            return jax.nn.relu(out)
        src, dst = (edge_index[0], edge_index[1])
        for l in range(L):
            x = _pna_layer(x, src, dst, edge_attr, edge_W[l], edge_b[l], pre_W[l], pre_b[l], post_W[l], post_b[l], lin_W[l], lin_b[l])
        return x
    edge_index = jnp.stack([src, dst])
    x = _layernorm(x + _L0_gnn_ref(x, edge_attr_32, L0_gnn_eps, src, dst), axis=-1)
    x = _layernorm(x + _L1_gnn_ref(x, L1_gnn_beta, src, dst), axis=-1)
    x = _layernorm(x + _L2_gnn_ref(x, edge_index, edge_attr_2, L2_gnn_weight, L2_gnn_root_weight, L2_gnn_bias), axis=-1)
    x = _layernorm(x + _L3_gnn_ref(x, edge_index, edge_attr_16, L3_gnn_edge_W, L3_gnn_edge_b, L3_gnn_pre_W, L3_gnn_pre_b, L3_gnn_post_W, L3_gnn_post_b, L3_gnn_lin_W, L3_gnn_lin_b), axis=-1)
    return x

_drawn_inputs = setup_inputs


def setup_inputs(seed=0):
    import zlib

    import numpy as np

    out = dict(_drawn_inputs(seed))
    spreads = {}
    factors = {'edge_attr_2': 8.0,
     'L2_gnn_weight': 8.0,
     'L2_gnn_bias': 3.762,
     'L3_gnn_post_b': 8.0,
     'L3_gnn_lin_b': 8.0}
    for name, (base, spread) in spreads.items():
        noise = np.random.default_rng([zlib.crc32(name.encode()), seed]).standard_normal(out[name].shape)
        drawn = base * np.exp(spread * noise) if base else spread * noise
        out[name] = jnp.asarray(drawn.astype(out[name].dtype))
    for name, factor in factors.items():
        out[name] = (out[name] * factor).astype(out[name].dtype)
    return out
```

```python
from contextlib import ExitStack

import concourse.bass as bass
from concourse import mybir

F32 = mybir.dt.float32
I32 = mybir.dt.int32
BF16 = mybir.dt.bfloat16
ALU = mybir.AluOpType
ACT = mybir.ActivationFunctionType
AXX = mybir.AxisListType.X

NN = 6250
NC = 49
NP = 128 * NC
E = 200000
J = 1568
NE = 128 * J
C = 56
NCH = J // C
H = 28
NG = J // H
BIG = 3.0e38
ENG = ("sync", "scalar", "vector", "tensor", "gpsimd")


class Done:

    def __init__(self, eng, phase):
        self.eng, self.phase, self.used, self.value = eng, phase, False, None


class Chan:

    def __init__(self, sem):
        self.sem, self.n = sem, 0


class Queues:

    def __init__(self, nc, ctx):
        self.nc, self.ctx = nc, ctx
        self.q = {e: [] for e in ENG}
        self.phase = 0
        self.chans = {}

    def chan(self, name):
        if name not in self.chans:
            self.chans[name] = Chan(self.ctx.enter_context(self.nc.semaphore("d_" + name)))
        return self.chans[name]

    def do(self, eng, fn, *after):
        d = Done(eng, self.phase)
        self._after(after)
        self.q[eng].append((fn, after, d, None))
        return d

    def dma(self, eng, fn, ch, *after):
        ch = self.chan(ch)
        ch.n += 16
        self._after(after)
        self.q[eng].append((fn, after, None, ch))
        return (ch, ch.n)

    def _after(self, after):
        for a in after:
            if isinstance(a, Done):
                a.used = True

    def step(self):
        self.phase += 1

    def meet(self):
        last = []
        for e in ENG:
            real = [d for fn, _, d, _ in self.q[e] if fn is not None and d is not None]
            if real:
                real[-1].used = True
                last.append(real[-1])
        for e in ENG:
            self.q[e].append((None, tuple(last), None, None))
        self.step()

    def emit(self):
        sems, count = {}, {}
        for e in ENG:
            for fn, after, d, ch in self.q[e]:
                if d is not None and d.used:
                    key = (e, d.phase)
                    if key not in sems:
                        sems[key] = self.ctx.enter_context(self.nc.semaphore(f"e_{e}_{d.phase}"))
                    count[key] = count.get(key, 0) + 1
                    d.value = count[key]
        block = self.ctx.enter_context(self.nc.Block())
        for e in ENG:
            getattr_block = {"sync": block.sync, "scalar": block.scalar, "vector": block.vector,
                             "tensor": block.tensor, "gpsimd": block.gpsimd}[e]

            def body(eng, e=e):
                seen = {}
                for fn, after, d, ch in self.q[e]:
                    need = {}
                    for a in after:
                        if a is None:
                            continue
                        if isinstance(a, Done):
                            key, sem, v = (a.eng, a.phase), sems[(a.eng, a.phase)], a.value
                        else:
                            key, sem, v = id(a[0]), a[0].sem, a[1]
                        if v > need.get(key, (None, 0))[1]:
                            need[key] = (sem, v)
                    for key, (sem, v) in need.items():
                        if v > seen.get(key, 0):
                            eng.wait_ge(sem, v)
                            seen[key] = v
                    if fn is None:
                        if d is not None and d.used:
                            eng.sem_inc(sems[(e, d.phase)], 1)
                        continue
                    ins = fn(eng)
                    if ch is not None:
                        ins.then_inc(ch.sem, 16)
                    elif d.used:
                        ins.then_inc(sems[(e, d.phase)], 1)

            getattr_block(body)


def program(nc, x, src, dst, ea16, ea2, ea32, eps, beta, w2, root2, bias2,
            eW, eb, pW, pb, poW, pob, lW, lb, out):
    ctx = ExitStack()
    with ctx:
        ctx.enter_context(nc.allow_non_contiguous_dma(reason="small weights, flags and index rows"))
        Q = Queues(nc, ctx)

        def V(fn, *after):
            return Q.do("vector", fn, *after)

        def S(fn, *after):
            return Q.do("scalar", fn, *after)

        def T(fn, *after):
            return Q.do("tensor", fn, *after)

        def G(fn, *after):
            return Q.do("gpsimd", fn, *after)

        def load(o, i, ch, *after, eng="sync"):
            return Q.dma(eng, lambda e: e.dma_start(o, i), ch, *after)

        def gather(o, table, idx, ch, *after):
            return Q.dma("gpsimd", lambda e: e.indirect_dma_start(
                o, None, table, bass.IndirectOffsetOnAxis(ap=idx, axis=0)), ch, *after)

        def scatter(table, idx, i, ch, *after):
            return Q.dma("gpsimd", lambda e: e.indirect_dma_start(
                table, bass.IndirectOffsetOnAxis(ap=idx, axis=0), i, None), ch, *after)

        def dram(name, shape, dt=F32):
            return nc.dram_tensor(name, shape, dt, kind="Internal").ap()

        def sb(st, name, shape, dt=F32):
            return st.enter_context(nc.sbuf_tensor(name, shape, dt))

        U = {"src": dram("U_src", [NE, 1], I32), "dst": dram("U_dst", [NE, 1], I32),
             "a2": dram("U_a2", [NE, 2]), "a16": dram("U_a16", [NE, 16]), "a32": dram("U_a32", [NE, 32])}
        R = dram("R", [NE, 52])
        KT = dram("KT", [J, 128], BF16)
        T0 = dram("T0", [NP, 32])
        T1 = dram("T1", [NP, 33])
        NH = dram("NH", [NP, 32])
        Y = dram("Y", [NP * 16, 128])
        TQ = dram("TQ", [NP, 32])
        S0 = dram("S0", [NE + NP, 32])
        T4 = dram("T4", [NE, 4], I32)
        W0 = dram("W0", [NE + 16, 32])
        W1 = dram("W1", [NE + 16, 34])
        W2 = dram("W2", [NE + 16, 32])
        W3 = dram("W3", [NE + 16, 64])

        ps = [ctx.enter_context(nc.psum_tensor(f"ps{i}", [128, 512], F32)) for i in range(8)]

        ident = sb(ctx, "ident", [128, 128])
        slt = sb(ctx, "slt", [128, 128])
        trib = sb(ctx, "trib", [128, 128], BF16)
        iot = sb(ctx, "iot", [128, 128], BF16)
        ioti = sb(ctx, "ioti", [128, 128], I32)
        iotp = sb(ctx, "iotp", [128, 1])
        iotpi = sb(ctx, "iotpi", [128, 1], I32)
        nodei = sb(ctx, "nodei", [128, NC], I32)
        nodef = sb(ctx, "nodef", [128, NC])
        zer = sb(ctx, "zer", [128, 1024])
        padi = sb(ctx, "padi", [64, 11], I32)
        X = sb(ctx, "X", [128, NC, 32])
        cnt = sb(ctx, "cnt", [128, NC])
        first = sb(ctx, "first", [128, NC])
        lastq = sb(ctx, "lastq", [128, NC], I32)
        startq = sb(ctx, "startq", [128, NC], I32)
        srcs = sb(ctx, "srcs", [128, J], I32)
        m01 = sb(ctx, "m01", [128, J])
        mneg = sb(ctx, "mneg", [128, J])
        pe = sb(ctx, "pe", [128, 4])
        feq = sb(ctx, "feq", [128, 1], I32)
        k0i = sb(ctx, "k0i", [128, 1], I32)
        cs = sb(ctx, "cnts", [128, NC])
        contT = sb(ctx, "contT", [64, 128])
        wT = sb(ctx, "wT", [64, 128])
        bcol = sb(ctx, "bcol", [128, 2])
        nd = sb(ctx, "nd", [128, NC, 32])
        nd2 = sb(ctx, "nd2", [128, NC, 32])
        st = sb(ctx, "st", [128, 4, NC])

        g0 = G(lambda e: e.memset(ident[:, :], 0.0))
        g1 = G(lambda e: e.affine_select(out=ident[:, :], in_=ident[:, :], compare_op=ALU.not_equal,
                                         fill=1.0, base=0, pattern=[[-1, 128]], channel_multiplier=1), g0)
        g2 = G(lambda e: e.memset(slt[:, :], 1.0), g1)
        g3 = G(lambda e: e.affine_select(out=slt[:, :], in_=slt[:, :], compare_op=ALU.is_gt,
                                         fill=0.0, base=0, pattern=[[1, 128]], channel_multiplier=-1), g2)
        g4 = G(lambda e: e.iota(ioti[:, :], [[1, 128]], base=0, channel_multiplier=0), g3)
        g5 = G(lambda e: e.iota(iotpi[:, :], [[0, 1]], base=0, channel_multiplier=1), g4)
        g6 = G(lambda e: e.iota(nodei[:, :], [[1, NC]], base=0, channel_multiplier=NC), g5)
        g7 = G(lambda e: e.memset(padi[:, :], NP - 1), g6)
        g8 = G(lambda e: e.memset(zer[:, :], 0.0), g7)
        V(lambda e: e.tensor_copy(trib[:, :], slt[:, :]), g3)
        V(lambda e: e.tensor_copy(iot[:, :], ioti[:, :]), g4)
        V(lambda e: e.tensor_copy(iotp[:, :], iotpi[:, :]), g5)
        V(lambda e: e.tensor_copy(nodef[:, :], nodei[:, :]), g6)

        ci = []
        ci.append(load(U["src"][0:E, 0].rearrange("(a b) -> a b", a=16), src.rearrange("(a b) -> a b", a=16), "ci"))
        ci.append(load(U["dst"][0:E, 0].rearrange("(a b) -> a b", a=16), dst.rearrange("(a b) -> a b", a=16), "ci"))
        for k, a in (("a2", ea2), ("a16", ea16), ("a32", ea32)):
            ci.append(load(U[k][0:E, :].rearrange("(a b) f -> a (b f)", a=64), a.rearrange("(a b) f -> a (b f)", a=64), "ci"))
            n = U[k].shape[1]
            ci.append(load(U[k][E:NE, :].rearrange("(a b) f -> a (b f)", a=64), zer[0:64, 0:11 * n], "ci", g8))
        for k in ("src", "dst"):
            ci.append(load(U[k][E:NE, 0].rearrange("(a b) -> a b", a=64), padi[:, :], "ci", g7))
        ci.append(load(T0[0:NN, :].rearrange("(a b) f -> a (b f)", a=125), x.rearrange("(a b) f -> a (b f)", a=125), "ci"))
        ci.append(load(T0[NN:NP, :], zer[0:22, 0:32], "ci", g8))
        for w in (W0, W1, W2, W3):
            ci.append(load(w[NE:NE + 16, :], zer[0:16, 0:w.shape[1]], "ci", g8))
        ci.append(load(bcol[:, 0:1], eps.rearrange("(a b) -> a b", a=1).to_broadcast([128, 1]), "ci"))
        ci.append(load(bcol[:, 1:2], beta.rearrange("(a b) -> a b", a=1).to_broadcast([128, 1]), "ci"))
        inputs_in = ci[-1]
        zs = None
        S0v = S0[0:NE, :].rearrange("(p j) f -> p (j f)", p=128)
        for k in range(NE * 32 // 128 // 1024):
            zs = load(S0v[:, k * 1024:(k + 1) * 1024], zer[:, :], "zs", g8, eng="scalar")
        starts_zeroed = zs
        x_in = load(X[:, :, :], T0.rearrange("(p c) f -> p c f", p=128), "xin", inputs_in)
        Q.meet()

        def rank(tag, key_dram, ready, cnt_t, first_t, pos, rows=None):
            with ExitStack() as st_:
                Kf = sb(st_, tag + "Kf", [128, J])
                lo = sb(st_, tag + "lo", [128, J])
                hib = sb(st_, tag + "hib", [128, J], BF16)
                lob = sb(st_, tag + "lob", [128, J], BF16)
                Ki = sb(st_, tag + "Ki", [128, J], I32)
                ktb = [sb(st_, tag + f"ktb{i}", [128, 128], BF16) for i in range(2)]
                AL = [sb(st_, tag + f"AL{i}", [128, H, 128], BF16) for i in range(2)]
                AH = [sb(st_, tag + f"AH{i}", [128, H, NC], BF16) for i in range(2)]
                AT = [sb(st_, tag + f"AT{i}", [128, H, 128]) for i in range(2)]
                EQ = sb(st_, tag + "EQ", [128, H, 128], BF16)
                M1 = [sb(st_, tag + f"M1{i}", [128, H, 128], BF16) for i in range(2)]
                LB = [sb(st_, tag + f"LB{i}", [128, H, 128], BF16) for i in range(2)]
                Cs = [sb(st_, tag + f"Cs{i}", [128, NC]) for i in range(2)]
                pr = sb(st_, tag + "pr", [128, 7, NC])
                rs = sb(st_, tag + "rs", [128, 2])
                rk = sb(st_, tag + "rk", [128, J])
                ex = sb(st_, tag + "ex", [128, NC + 1])
                kin = load(Ki[:, :], key_dram[:, 0].rearrange("(p j) -> p j", p=128), tag + "ki", ready)
                a = V(lambda e: e.tensor_copy(Kf[:, :], Ki[:, :]), kin)
                a = V(lambda e: e.tensor_scalar(Ki[:, :], Kf[:, :], 1.0 / 49, 0.5 / 49, ALU.mult, ALU.add), a)
                a = V(lambda e: e.tensor_copy(lo[:, :], Ki[:, :]), a)
                a = V(lambda e: e.scalar_tensor_tensor(out=rk[:, :], in0=lo[:, :], scalar=-49.0, in1=Kf[:, :],
                                                       op0=ALU.mult, op1=ALU.add), a)
                a = V(lambda e: e.tensor_scalar(Kf[:, :], rk[:, :], 0.0, None, ALU.is_lt), a)
                b = V(lambda e: e.tensor_tensor(lo[:, :], lo[:, :], Kf[:, :], ALU.subtract), a)
                hi_ok = V(lambda e: e.scalar_tensor_tensor(out=hib[:, :], in0=Kf[:, :], scalar=49.0, in1=rk[:, :],
                                                           op0=ALU.mult, op1=ALU.add), b)
                lo_ok = V(lambda e: e.tensor_copy(lob[:, :], lo[:, :]), b)

                wr, cp = [None, None], []
                for i in range(13):
                    w = min(128, J - 128 * i)
                    t = T(lambda e, i=i, w=w: e.transpose(ps[i % 2][0:w, 0:128], lo[:, 128 * i:128 * i + w], ident[:, :]),
                          b, cp[i - 2] if i >= 2 else None)
                    cp.append(S(lambda e, i=i, w=w: e.copy(ktb[i % 2][0:w, :], ps[i % 2][0:w, 0:128]), t, wr[i % 2]))
                    wr[i % 2] = load(KT[128 * i:128 * i + w, :], ktb[i % 2][0:w, :], tag + f"kt{i % 2}", cp[-1])
                kt_out = wr

                used = [None, None]
                for g in range(NG):
                    s = g % 2
                    h = V(lambda e, g=g, s=s: e.tensor_tensor(
                        AH[s][:, :, :], iot[:, None, 0:NC].to_broadcast([128, H, NC]),
                        hib[:, g * H:(g + 1) * H, None].to_broadcast([128, H, NC]), ALU.is_equal), hi_ok, used[s])
                    h = V(lambda e, g=g, s=s: e.tensor_tensor(
                        AL[s][:, :, :], iot[:, None, :].to_broadcast([128, H, 128]),
                        lob[:, g * H:(g + 1) * H, None].to_broadcast([128, H, 128]), ALU.is_equal), lo_ok, used[s])
                    for j in range(H):
                        used[s] = T(lambda e, g=g, s=s, j=j: e.matmul(
                            ps[2][:, 0:NC], AL[s][:, j, :], AH[s][:, j, :], start=(g == 0 and j == 0),
                            stop=(g == NG - 1 and j == H - 1)), h)
                a = V(lambda e: e.tensor_copy(cnt_t[:, :], ps[2][:, 0:NC]), used[(NG - 1) % 2])
                z = V(lambda e: e.memset(ex[:, :], 0.0))
                a = V(lambda e: e.tensor_tensor_scan(ex[:, 1:NC + 1], cnt_t[:, :], cnt_t[:, :], 0.0,
                                                     ALU.add, ALU.bypass), a, z)
                t = T(lambda e: e.matmul(ps[3][:, 0:1], slt[:, :], ex[:, NC:NC + 1], start=True, stop=True), a)
                a = V(lambda e: e.tensor_copy(rs[:, 0:1], ps[3][:, 0:1]), t)
                fst = V(lambda e: e.tensor_scalar(first_t[:, :], ex[:, 0:NC], rs[:, 0:1], None, ALU.add), a)
                if pos is None:
                    return fst

                t0 = T(lambda e: e.matmul(ps[2][:, 0:NC], ident[:, :], first_t[:, :], start=True, stop=False,
                                          skip_group_check=True), fst)
                hist = t0
                lbd = [None, None]
                red = [None, None]
                csr = [None, None]
                rd, h4 = None, None
                for g in range(NG):
                    s = g % 2
                    ld = load(LB[s][:, :, :], KT[g * H:(g + 1) * H, :].rearrange("(o j) p -> o j p", o=1)
                              .to_broadcast([128, H, 128]), tag + f"lb{s}", lbd[s], *kt_out)
                    h0 = V(lambda e, g=g, s=s: e.tensor_tensor(
                        AH[s][:, :, :], iot[:, None, 0:NC].to_broadcast([128, H, NC]),
                        hib[:, g * H:(g + 1) * H, None].to_broadcast([128, H, NC]), ALU.is_equal), used[s])
                    h1 = V(lambda e, g=g, s=s: e.tensor_tensor(
                        AL[s][:, :, :], iot[:, None, :].to_broadcast([128, H, 128]),
                        lob[:, g * H:(g + 1) * H, None].to_broadcast([128, H, 128]), ALU.is_equal), used[s])
                    h2 = V(lambda e, s=s: e.tensor_scalar(AT[s][:, :, :], LB[s][:, :, :], iotp[:, 0:1], None,
                                                          ALU.is_equal), ld, used[s])
                    h3 = V(lambda e, g=g, s=s: e.tensor_tensor(
                        EQ[:, :, :], LB[s][:, :, :],
                        lob[:, g * H:(g + 1) * H, None].to_broadcast([128, H, 128]), ALU.is_equal), ld, h4)
                    lbd[s] = h3
                    h4 = V(lambda e, s=s: e.tensor_tensor(M1[s][:, :, :], EQ[:, :, :],
                                                          trib[:, None, :].to_broadcast([128, H, 128]), ALU.mult),
                           h3, used[s])
                    for j in range(H):
                        i = g * H + j
                        bank = 4 + (i // 7) % 2
                        o = 0 + NC * (i % 7)
                        cs = S(lambda e, i=i: e.copy(Cs[i % 2][:, :], ps[2][:, 0:NC]), hist, csr[i % 2])
                        lk = T(lambda e, s=s, j=j, i=i, bank=bank, o=o: e.matmul(
                            ps[bank][:, o:o + NC], AT[s][:, j, :], Cs[i % 2][:, :], start=True, stop=False,
                            skip_group_check=True), cs, h2, red[(i // 7) % 2])
                        csr[i % 2] = lk
                        lk = T(lambda e, s=s, j=j, bank=bank, o=o: e.matmul(
                            ps[bank][:, o:o + NC], M1[s][:, j, :], AH[s][:, j, :], start=False, stop=True,
                            skip_group_check=True), h4, h0)
                        hist = T(lambda e, s=s, j=j: e.matmul(
                            ps[2][:, 0:NC], AL[s][:, j, :], AH[s][:, j, :], start=False, stop=False,
                            skip_group_check=True), h1, h0, cs)
                        if i % 7 == 6:
                            pd = V(lambda e, s=s, j=j, bank=bank: e.tensor_tensor(
                                pr[:, :, :], ps[bank][:, 0:7 * NC].rearrange("p (a b) -> p a b", a=7),
                                AH[s][:, j - 6:j + 1, :], ALU.mult), lk, rd)
                            rd = V(lambda e, i=i: e.tensor_reduce(rk[:, i - 6:i + 1], pr[:, :, :], AXX, ALU.add), pd)
                            red[(i // 7) % 2] = rd
                    used[s] = V(None, rd, hist)
                return V(lambda e: e.tensor_copy(pos[:, :], rk[:, :]), rd)

        known = {}

        def sort_by_dst():
            with ExitStack() as ph:
                pos = sb(ph, "posd", [128, J], I32)
                with ExitStack() as ph2:
                    ranked = rank("a", U["dst"], inputs_in, cnt, first, pos)
                Q.meet()
                with ExitStack() as ph2:
                    pay = [sb(ph2, f"pay{i}", [128, C, 52]) for i in range(2)]
                    b32 = [sb(ph2, f"b32_{i}", [128, C, 32]) for i in range(2)]
                    b16 = [sb(ph2, f"b16_{i}", [128, C, 16]) for i in range(2)]
                    bsm = [sb(ph2, f"bsm_{i}", [128, C, 4]) for i in range(2)]
                    bi = [sb(ph2, f"bi_{i}", [128, 2, C], I32) for i in range(2)]
                    sc = [None, None]
                    cpd = [None, None]
                    for c in range(NCH):
                        s = c % 2
                        v = {k: U[k].rearrange("(p j) f -> p j f", p=128)[:, c * C:(c + 1) * C, :] for k in U}
                        load(b32[s][:, :, :], v["a32"], f"pl{s}", cpd[s])
                        load(b16[s][:, :, :], v["a16"], f"pl{s}")
                        load(bsm[s][:, :, 0:2], v["a2"], f"pl{s}")
                        load(bi[s][:, 0, :], v["src"].rearrange("p j f -> p (j f)"), f"pl{s}")
                        l = load(bi[s][:, 1, :], v["dst"].rearrange("p j f -> p (j f)"), f"pl{s}")
                        a = V(lambda e, s=s: e.tensor_copy(pay[s][:, :, 0:32], b32[s][:, :, :]), l, sc[s])
                        a = V(lambda e, s=s: e.tensor_copy(pay[s][:, :, 32:48], b16[s][:, :, :]), l)
                        a = V(lambda e, s=s: e.tensor_copy(pay[s][:, :, 48:50], bsm[s][:, :, 0:2]), l)
                        a = V(lambda e, s=s: e.tensor_copy(pay[s][:, :, 50:52].bitcast(I32),
                                                           bi[s][:, :, :].rearrange("p k j -> p j k")), l)
                        cpd[s] = a
                        for j in range(C):
                            sc[s] = scatter(R, pos[:, c * C + j:c * C + j + 1], pay[s][:, j, :], f"sc{s}", a, ranked)
                    scattered = sc
                Q.meet()
                with ExitStack() as ph2:
                    pay_o = [sb(ph2, f"qay{i}", [128, C, 52]) for i in range(2)]
                    b32_o = [sb(ph2, f"c32_{i}", [128, C, 32]) for i in range(2)]
                    b16_o = [sb(ph2, f"c16_{i}", [128, C, 16]) for i in range(2)]
                    b2 = [sb(ph2, f"c2_{i}", [128, C, 2]) for i in range(2)]
                    bi_o = [sb(ph2, f"ci_{i}", [128, 2, C], I32) for i in range(2)]
                    stq = [None, None]
                    cpd = [None, None]
                    for c in range(NCH):
                        s = c % 2
                        v = {k: U[k].rearrange("(p j) f -> p j f", p=128)[:, c * C:(c + 1) * C, :] for k in U}
                        l = load(pay_o[s][:, :, :], R.rearrange("(p j) f -> p j f", p=128)[:, c * C:(c + 1) * C, :],
                                 f"ql{s}", cpd[s], *scattered)
                        V(lambda e, s=s: e.tensor_copy(b32_o[s][:, :, :], pay_o[s][:, :, 0:32]), l, stq[s])
                        V(lambda e, s=s: e.tensor_copy(b16_o[s][:, :, :], pay_o[s][:, :, 32:48]), l)
                        V(lambda e, s=s: e.tensor_copy(b2[s][:, :, :], pay_o[s][:, :, 48:50]), l)
                        a = V(lambda e, s=s: e.tensor_copy(bi_o[s][:, :, :].rearrange("p k j -> p j k"),
                                                           pay_o[s][:, :, 50:52].bitcast(I32)), l)
                        cpd[s] = a
                        load(v["a32"], b32_o[s][:, :, :], f"qs{s}", a)
                        load(v["a16"], b16_o[s][:, :, :], f"qs{s}")
                        load(v["a2"], b2[s][:, :, :], f"qs{s}")
                        load(v["src"].rearrange("p j f -> p (j f)"), bi_o[s][:, 0, :], f"qs{s}")
                        stq[s] = load(v["dst"].rearrange("p j f -> p (j f)"), bi_o[s][:, 1, :], f"qs{s}")
                    known["sorted_in"] = stq
                Q.meet()

        sort_by_dst()

        def segments(tag, key_f, prev_last, ready, m01_t, mneg_t, cnt_t, first_t, last_t, start_t, pe_t, feq_t,
                     cT, wTt):
            with ExitStack() as st_:
                q = sb(st_, tag + "q", [128, J])
                fl = sb(st_, tag + "fl", [128, 4])
                nf = sb(st_, tag + "nf", [128, NC])
                nf2 = sb(st_, tag + "nf2", [128, NC])
                a = V(lambda e: e.memset(m01_t[:, 0:1], 0.0))
                a = V(lambda e: e.tensor_tensor(m01_t[:, 1:J], key_f[:, 1:J], key_f[:, 0:J - 1], ALU.is_equal), a, ready)
                if mneg_t is not None:
                    V(lambda e: e.tensor_scalar(mneg_t[:, :], m01_t[:, :], -1.0, BIG, ALU.add, ALU.mult), a)
                a = V(lambda e: e.tensor_scalar(q[:, :], key_f[:, :], key_f[:, 0:1], None, ALU.is_equal), ready)
                a = V(lambda e: e.tensor_reduce(fl[:, 0:1], q[:, :], AXX, ALU.add), a)
                b = V(lambda e: e.scalar_tensor_tensor(out=fl[:, 1:2], in0=iotp[:, 0:1], scalar=float(J),
                                                       in1=fl[:, 0:1], op0=ALU.mult, op1=ALU.add), a)
                b = V(lambda e: e.tensor_scalar(feq_t[:, :], fl[:, 1:2], -1.0, None, ALU.add), b)
                c = V(lambda e: e.tensor_tensor(pe_t[:, 0:1], key_f[:, 0:1], prev_last[:, 0:1], ALU.is_equal), ready)
                d = V(lambda e: e.tensor_scalar(fl[:, 2:3], fl[:, 0:1], float(J), None, ALU.is_ge), a)
                c = V(lambda e: e.tensor_tensor(pe_t[:, 1:2], pe_t[:, 0:1], fl[:, 2:3], ALU.mult), c, d)
                t1 = T(lambda e: e.matmul(ps[6][0:64, 0:128], pe_t[:, 0:1].to_broadcast([128, 64]), ident[:, :],
                                          start=True, stop=True), c)
                t2 = T(lambda e: e.matmul(ps[7][0:64, 0:128], pe_t[:, 1:2].to_broadcast([128, 64]), ident[:, :],
                                          start=True, stop=True), c)
                V(lambda e: e.tensor_copy(cT[:, :], ps[6][0:64, 0:128]), t1)
                V(lambda e: e.tensor_copy(wTt[:, :], ps[7][0:64, 0:128]), t2)
                h = V(lambda e: e.tensor_scalar(nf[:, :], cnt_t[:, :], 0.0, None, ALU.is_gt))
                i = V(lambda e: e.tensor_tensor(nf2[:, :], first_t[:, :], cnt_t[:, :], ALU.add))
                i = V(lambda e: e.tensor_scalar(nf2[:, :], nf2[:, :], -1.0 - NE, None, ALU.add), i)
                i = V(lambda e: e.tensor_tensor(nf2[:, :], nf2[:, :], nf[:, :], ALU.mult), h, i)
                i = V(lambda e: e.tensor_scalar(last_t[:, :], nf2[:, :], float(NE), None, ALU.add), i)
                if start_t is not None:
                    i = V(lambda e: e.tensor_tensor(nf2[:, :], first_t[:, :], nodef[:, :], ALU.subtract), i)
                    i = V(lambda e: e.tensor_scalar(nf2[:, :], nf2[:, :], -float(NE), None, ALU.add), i)
                    i = V(lambda e: e.tensor_tensor(nf2[:, :], nf2[:, :], nf[:, :], ALU.mult), i)
                    i = V(lambda e: e.tensor_tensor(nf2[:, :], nf2[:, :], nodef[:, :], ALU.add), i)
                    i = V(lambda e: e.tensor_scalar(start_t[:, :], nf2[:, :], float(NE), None, ALU.add), i)
                return V(None, i, b)

        def dst_segments():
            with ExitStack() as ph:
                ki = sb(ph, "ki", [128, J], I32)
                kf = sb(ph, "kf", [128, J])
                pli = sb(ph, "pli", [128, 1], I32)
                plf = sb(ph, "plf", [128, 1])
                keyflat = U["dst"][:, 0]
                l = load(ki[:, :], keyflat.rearrange("(p j) -> p j", p=128), "k1", *known["sorted_in"])
                load(srcs[:, :], U["src"][:, 0].rearrange("(p j) -> p j", p=128), "k1")
                z = V(lambda e: e.memset(pli[:, :], -1))
                l = load(pli[1:128, :], keyflat.rearrange("(p j) -> p j", p=128)[0:127, J - 1:J], "k1", z)
                a = V(lambda e: e.tensor_copy(kf[:, :], ki[:, :]), l)
                b = V(lambda e: e.tensor_copy(plf[:, :], pli[:, :]), l)
                V(lambda e: e.tensor_copy(k0i[:, :], ki[:, 0:1]), l)
                c = V(None, a, b)
                known["seg"] = segments("sa", kf, plf, c, m01, mneg, cnt, first, lastq, startq, pe, feq, contT, wT)

        dst_segments()
        Q.meet()

        def scans(o, data0, data1, init, width, op0, op1, *after):
            last = None
            for f in range(width):
                ini = init(f)
                last = V(lambda e, f=f, ini=ini: e.tensor_tensor_scan(o(f), data0, data1(f), ini, op0, op1), *after)
            return last

        def layernorm(y, sq, o, *after):
            mu, var = st[:, 0, :], st[:, 1, :]
            a = V(lambda e: e.tensor_reduce(mu, y[:, :, :], AXX, ALU.add), *after)
            a = V(lambda e: e.tensor_scalar(mu, mu, 1.0 / 32, None, ALU.mult), a)
            a = V(lambda e: e.tensor_tensor(y[:, :, :], y[:, :, :], mu[:, :, None].to_broadcast([128, NC, 32]),
                                            ALU.subtract), a)
            b = V(lambda e: e.tensor_tensor(sq[:, :, :], y[:, :, :], y[:, :, :], ALU.mult), a)
            b = V(lambda e: e.tensor_reduce(var, sq[:, :, :], AXX, ALU.add), b)
            b = V(lambda e: e.tensor_scalar(var, var, 1.0 / 32, 1e-5, ALU.mult, ALU.add), b)
            c = S(lambda e: e.activation(var, var, ACT.Sqrt), b)
            c = V(lambda e: e.reciprocal(var, var), c)
            return V(lambda e: e.tensor_tensor(o[:, :, :], y[:, :, :], var[:, :, None].to_broadcast([128, NC, 32]),
                                               ALU.mult), c)

        def node_view(t):
            return t.rearrange("(p c) f -> p c f", p=128)

        def node_gather(o, table, idx, tag, *after):
            t = None
            for c in range(NC):
                t = gather(o[:, c, :], table, idx[:, c:c + 1], tag, *after)
            return t

        def fixup_sum(tag, lastcol, width, kind, table, feq_t, cT, wTt, stored, ready):
            with ExitStack() as st_:
                eT = sb(st_, tag + "eT", [64, 128])
                sT = sb(st_, tag + "sT", [64, 128])
                cTr = sb(st_, tag + "cT", [64, 128])
                wn = sb(st_, tag + "wn", [64, 128])
                cn = sb(st_, tag + "cn", [64, 128])
                row = sb(st_, tag + "row", [128, 64])
                row2 = sb(st_, tag + "row2", [128, 64])
                t = T(lambda e: e.transpose(ps[6][0:width, 0:128], lastcol, ident[:, :]), ready)
                a = V(lambda e: e.tensor_copy(eT[0:width, :], ps[6][0:width, 0:128]), t)
                b = V(lambda e: e.tensor_scalar(wn[:, :], wTt[:, :], -1.0, BIG, ALU.add, ALU.mult))
                b = V(lambda e: e.tensor_scalar(cn[:, :], cT[:, :], -1.0, BIG, ALU.add, ALU.mult))
                m = V(lambda e: e.memset(cTr[:, :], 0.0))
                c = None
                for f0, f1, mx in kind:
                    d0 = wn if mx else wTt
                    c = V(lambda e, f0=f0, f1=f1, d0=d0, mx=mx: e.tensor_tensor_scan(
                        sT[f0:f1, :], d0[f0:f1, :], eT[f0:f1, :], -BIG if mx else 0.0,
                        ALU.add if mx else ALU.mult, ALU.max if mx else ALU.add), a, b)
                    if mx:
                        m = V(lambda e, f0=f0, f1=f1: e.memset(cTr[f0:f1, 0:1], -BIG), m)
                    c = V(lambda e, f0=f0, f1=f1, mx=mx: e.tensor_tensor(
                        cTr[f0:f1, 1:128], sT[f0:f1, 0:127], (cn if mx else cT)[f0:f1, 1:128],
                        ALU.add if mx else ALU.mult), c, m)
                t = T(lambda e: e.transpose(ps[7][:, 0:width], cTr[0:width, :], ident[0:width, 0:width]), c, m)
                g = gather(row[:, 0:width], table, feq_t[:, 0:1], "fx", *stored)
                for f0, f1, mx in kind:
                    c = V(lambda e, f0=f0, f1=f1, mx=mx: e.tensor_tensor(
                        row2[:, f0:f1], row[:, f0:f1], ps[7][:, f0:f1], ALU.max if mx else ALU.add), t, g)
                return scatter(table, feq_t[:, 0:1], row2[:, 0:width], "fx", c)

        def layer0():
            with ExitStack() as ph:
                Gb = [sb(ph, f"l0g{i}", [128, C, 32]) for i in range(3)]
                Ea = [sb(ph, f"l0e{i}", [128, C, 32]) for i in range(2)]
                Vb = [sb(ph, f"l0v{i}", [128, C, 32]) for i in range(2)]
                O = [sb(ph, f"l0o{i}", [128, C, 32]) for i in range(2)]
                addd, rel, scd, stq = [None] * NCH, [None] * NCH, [None] * NCH, [None] * NCH
                for c in range(NCH):
                    s, s3 = c % 2, c % 3
                    for j in range(C):
                        g = gather(Gb[s3][:, j, :], T0, srcs[:, c * C + j:c * C + j + 1], f"l0g{s3}",
                                   addd[c - 3] if c >= 3 else None)
                    l = load(Ea[s][:, :, :], U["a32"].rearrange("(p j) f -> p j f", p=128)[:, c * C:(c + 1) * C, :],
                             f"l0e{s}", addd[c - 2] if c >= 2 else None)
                    addd[c] = V(lambda e, s=s, s3=s3: e.tensor_tensor(Vb[s][:, :, :], Gb[s3][:, :, :], Ea[s][:, :, :],
                                                                      ALU.add), g, l, scd[c - 2] if c >= 2 else None)
                    rel[c] = S(lambda e, s=s: e.activation(Vb[s][:, :, :], Vb[s][:, :, :], ACT.Relu), addd[c])
                    scd[c] = scans(lambda f, s=s: O[s][:, :, f], m01[:, c * C:(c + 1) * C],
                                   lambda f, s=s: Vb[s][:, :, f],
                                   (lambda f: 0.0) if c == 0 else (lambda f, s=s: O[1 - s][:, C - 1, f:f + 1]),
                                   32, ALU.mult, ALU.add, rel[c], stq[c - 2] if c >= 2 else None,
                                   scd[c - 1] if c else None)
                    stq[c] = load(W0[0:NE, :].rearrange("(p j) f -> p j f", p=128)[:, c * C:(c + 1) * C, :],
                                  O[s][:, :, :], f"l0s{s}", scd[c])
                fx = fixup_sum("f0", O[(NCH - 1) % 2][:, C - 1, :], 32, [(0, 32, False)], W0, feq, contT, wT,
                               stq[-2:], scd[-1])
                ng = node_gather(nd, W0, lastq, "ng", fx)
                a = V(lambda e: e.tensor_scalar(st[:, 2, 0:1], bcol[:, 0:1], 2.0, None, ALU.add))
                a = V(lambda e: e.scalar_tensor_tensor(out=nd[:, :, :], in0=X[:, :, :], scalar=st[:, 2, 0:1],
                                                       in1=nd[:, :, :], op0=ALU.mult, op1=ALU.add), a, ng)
                x1 = layernorm(nd, nd2, X, a)

        layer0()
        Q.meet()

        def layer1():
            with ExitStack() as ph:
                TT = sb(ph, "l1t", [128, NC, 33])
                Gb = [sb(ph, f"l1g{i}", [128, C, 33]) for i in range(3)]
                Sb = [sb(ph, f"l1s{i}", [128, C, 32]) for i in range(2)]
                Db = [sb(ph, f"l1d{i}", [128, C, 32]) for i in range(2)]
                Pb = sb(ph, "l1p", [128, C, 33])
                O = [sb(ph, f"l1o{i}", [128, C, 34]) for i in range(2)]
                K0 = sb(ph, "l1k0", [128, 32])
                M = sb(ph, "l1m", [128, J + 1])
                ev = sb(ph, "l1e", [128, C])
                av = sb(ph, "l1a", [128, 2, C])
                a = V(lambda e: e.tensor_tensor(nd[:, :, :], X[:, :, :], X[:, :, :], ALU.mult))
                a = V(lambda e: e.tensor_reduce(st[:, 0, :], nd[:, :, :], AXX, ALU.add), a)
                a = S(lambda e: e.activation(st[:, 0, :], st[:, 0, :], ACT.Sqrt), a)
                a = V(lambda e: e.tensor_scalar(st[:, 0, :], st[:, 0, :], 1e-12, None, ALU.max), a)
                a = V(lambda e: e.reciprocal(st[:, 1, :], st[:, 0, :]), a)
                b = V(lambda e: e.tensor_copy(TT[:, :, 32], st[:, 1, :]), a)
                c_ = V(lambda e: e.tensor_copy(TT[:, :, 0:32], X[:, :, :]))
                b = load(node_view(T1), TT[:, :, :], "t1", b, c_)
                a = V(lambda e: e.tensor_scalar(st[:, 2, :], st[:, 1, :], bcol[:, 1:2], None, ALU.mult), a)
                a = V(lambda e: e.tensor_tensor(nd[:, :, :], X[:, :, :], st[:, 2, :, None].to_broadcast([128, NC, 32]),
                                                ALU.mult), a)
                d = load(node_view(NH), nd[:, :, :], "t1", a)
                k0 = gather(K0[:, :], NH, k0i[:, 0:1], "k0", d)
                ss = None
                for c in range(NC):
                    ss = scatter(S0, startq[:, c:c + 1], nd[:, c, :], "ss", a, starts_zeroed)
                mi = V(lambda e: e.memset(M[:, 0:1], -BIG))
                prod, fil, scd, stq, dd = [None] * NCH, [None] * NCH, [None] * NCH, [None] * NCH, [None] * NCH
                for c in range(NCH):
                    s, s3 = c % 2, c % 3
                    for j in range(C):
                        g = gather(Gb[s3][:, j, :], T1, srcs[:, c * C + j:c * C + j + 1], f"l1g{s3}", d,
                                   prod[c - 3] if c >= 3 else None)
                    l = load(Sb[s][:, :, :], S0v.rearrange("p (j f) -> p j f", f=32)[:, c * C:(c + 1) * C, :],
                             f"l1s{s}", fil[c - 2] if c >= 2 else None, ss)
                    if c == 0:
                        l = V(lambda e: e.tensor_copy(Sb[0][:, 0, :], K0[:, :]), l, k0)
                    fil[c] = scans(lambda f, s=s: Db[s][:, :, f], m01[:, c * C:(c + 1) * C],
                                   lambda f, s=s: Sb[s][:, :, f],
                                   (lambda f: 0.0) if c == 0 else (lambda f, s=s: Db[1 - s][:, C - 1, f:f + 1]),
                                   32, ALU.mult, ALU.add, l, dd[c - 1] if c else None, fil[c - 1] if c else None)
                    a = V(lambda e, s=s, s3=s3: e.tensor_tensor(Pb[:, :, 0:32], Gb[s3][:, :, 0:32], Db[s][:, :, :],
                                                                ALU.mult), g, fil[c], scd[c - 1] if c else None)
                    dd[c] = a
                    a = V(lambda e: e.tensor_reduce(ev[:, :], Pb[:, :, 0:32], AXX, ALU.add), a)
                    a = V(lambda e, s3=s3: e.tensor_tensor(ev[:, :], ev[:, :], Gb[s3][:, :, 32], ALU.mult), a)
                    a = V(lambda e, c=c: e.tensor_tensor_scan(M[:, 1 + c * C:1 + (c + 1) * C],
                                                              mneg[:, c * C:(c + 1) * C], ev[:, :],
                                                              M[:, c * C:c * C + 1], ALU.add, ALU.max), a, mi)
                    b = V(lambda e, c=c: e.tensor_tensor(ev[:, :], ev[:, :], M[:, 1 + c * C:1 + (c + 1) * C],
                                                         ALU.subtract), a)
                    m = V(lambda e, c=c: e.tensor_tensor(av[:, 0, :], M[:, c * C:(c + 1) * C],
                                                         M[:, 1 + c * C:1 + (c + 1) * C], ALU.subtract), a)
                    m = V(lambda e: e.tensor_scalar(av[:, 0, :], av[:, 0, :], 0.0, None, ALU.min), m)
                    b = S(lambda e: e.activation(ev[:, :], ev[:, :], ACT.Exp), b)
                    m = S(lambda e: e.activation(av[:, 0, :], av[:, 0, :], ACT.Exp), m)
                    m = V(lambda e, c=c: e.tensor_tensor(av[:, 1, :], av[:, 0, :], m01[:, c * C:(c + 1) * C],
                                                         ALU.mult), m)
                    n = V(lambda e, s3=s3: e.tensor_tensor(Pb[:, :, 0:32], Gb[s3][:, :, 0:32],
                                                           ev[:, :, None].to_broadcast([128, C, 32]), ALU.mult), b)
                    prod[c] = n
                    n = V(lambda e: e.tensor_copy(Pb[:, :, 32], ev[:, :]), n)
                    m = V(lambda e, c=c, s=s: e.tensor_copy(O[s][:, :, 33], M[:, 1 + c * C:1 + (c + 1) * C]), m,
                          stq[c - 2] if c >= 2 else None)
                    scd[c] = scans(lambda f, s=s: O[s][:, :, f], av[:, 1, :], lambda f: Pb[:, :, f],
                                   (lambda f: 0.0) if c == 0 else (lambda f, s=s: O[1 - s][:, C - 1, f:f + 1]),
                                   33, ALU.mult, ALU.add, n, m, scd[c - 1] if c else None)
                    stq[c] = load(W1[0:NE, :].rearrange("(p j) f -> p j f", p=128)[:, c * C:(c + 1) * C, :],
                                  O[s][:, :, :], f"l1o{s}", scd[c])
                fe = sb(ph, "l1fe", [33, 8, 128])
                row = sb(ph, "l1row", [128, 34])
                row2 = sb(ph, "l1row2", [128, 34])
                fs = sb(ph, "l1fs", [128, 8])
                OL = O[(NCH - 1) % 2]
                t1 = T(lambda e: e.transpose(ps[6][0:33, 0:128], OL[:, C - 1, 0:33], ident[:, :]), scd[-1])
                t2 = T(lambda e: e.matmul(ps[7][0:33, 0:128], OL[:, C - 1, 33:34].to_broadcast([128, 33]), ident[:, :],
                                          start=True, stop=True), scd[-1])
                a = V(lambda e: e.tensor_copy(fe[:, 0, :], ps[7][0:33, 0:128]), t2)
                a = V(lambda e: e.tensor_scalar(fe[:, 1, :], wT[0:33, :], -1.0, BIG, ALU.add, ALU.mult), a)
                b = V(lambda e: e.memset(fe[:, 2, :], -BIG))
                a = V(lambda e: e.tensor_tensor_scan(fe[:, 3, :], fe[:, 1, :], fe[:, 0, :], -BIG, ALU.add, ALU.max), a)
                b = V(lambda e: e.tensor_copy(fe[:, 2, 1:128], fe[:, 3, 0:127]), a, b)
                a = V(lambda e: e.tensor_tensor(fe[:, 0, :], fe[:, 0, :], fe[:, 3, :], ALU.subtract), a)
                a = S(lambda e: e.activation(fe[:, 0, :], fe[:, 0, :], ACT.Exp), a)
                a = V(lambda e: e.tensor_tensor(fe[:, 4, :], fe[:, 0, :], ps[6][0:33, 0:128], ALU.mult), a, t1)
                b = V(lambda e: e.tensor_tensor(fe[:, 5, :], fe[:, 2, :], fe[:, 3, :], ALU.subtract), b)
                b = V(lambda e: e.tensor_scalar(fe[:, 5, :], fe[:, 5, :], 0.0, None, ALU.min), b)
                b = S(lambda e: e.activation(fe[:, 5, :], fe[:, 5, :], ACT.Exp), b)
                b = V(lambda e: e.tensor_tensor(fe[:, 5, :], fe[:, 5, :], wT[0:33, :], ALU.mult), b)
                z = V(lambda e: e.memset(fe[:, 7, :], 0.0))
                a = V(lambda e: e.tensor_tensor_scan(fe[:, 6, :], fe[:, 5, :], fe[:, 4, :], 0.0, ALU.mult, ALU.add), a, b)
                a = V(lambda e: e.tensor_copy(fe[:, 7, 1:128], fe[:, 6, 0:127]), a, z)
                t1 = T(lambda e: e.transpose(ps[6][:, 0:33], fe[:, 7, :], ident[0:33, 0:33]), a)
                t2 = T(lambda e: e.transpose(ps[7][:, 0:33], fe[:, 2, :], ident[0:33, 0:33]), a)
                g = gather(row[:, :], W1, feq[:, 0:1], "fx", stq[-1], stq[-2])
                b = V(lambda e: e.tensor_scalar(fs[:, 4:5], pe[:, 0:1], -1.0, BIG, ALU.add, ALU.mult))
                b = V(lambda e: e.scalar_tensor_tensor(out=fs[:, 0:1], in0=ps[7][:, 0:1], scalar=pe[:, 0:1],
                                                   in1=fs[:, 4:5], op0=ALU.mult, op1=ALU.add), b, t2)
                b = V(lambda e: e.tensor_tensor(fs[:, 1:2], fs[:, 0:1], row[:, 33:34], ALU.max), b, g)
                c1 = V(lambda e: e.tensor_tensor(fs[:, 2:3], row[:, 33:34], fs[:, 1:2], ALU.subtract), b)
                c2 = V(lambda e: e.tensor_tensor(fs[:, 3:4], fs[:, 0:1], fs[:, 1:2], ALU.subtract), b)
                c1 = S(lambda e: e.activation(fs[:, 2:4], fs[:, 2:4], ACT.Exp), c1, c2)
                c2 = V(lambda e: e.tensor_tensor(fs[:, 3:4], fs[:, 3:4], pe[:, 0:1], ALU.mult), c1)
                d = V(lambda e: e.tensor_scalar(row2[:, 0:33], row[:, 0:33], fs[:, 2:3], None, ALU.mult), c1)
                d = V(lambda e: e.scalar_tensor_tensor(out=row2[:, 0:33], in0=ps[6][:, 0:33], scalar=fs[:, 3:4],
                                                       in1=row2[:, 0:33], op0=ALU.mult, op1=ALU.add), d, c2, t1)
                d2 = V(lambda e: e.tensor_copy(row2[:, 33:34], fs[:, 1:2]), b)
                fx = scatter(W1, feq[:, 0:1], row2[:, :], "fx", d, d2)
                NB = sb(ph, "l1n", [128, NC, 34])
                ng = node_gather(NB, W1, lastq, "ng", fx)
                a = V(lambda e: e.tensor_scalar(st[:, 0, :], NB[:, :, 32], 1e-30, None, ALU.max), ng)
                a = V(lambda e: e.reciprocal(st[:, 0, :], st[:, 0, :]), a)
                a = V(lambda e: e.tensor_tensor(nd[:, :, :], NB[:, :, 0:32], st[:, 0, :, None].to_broadcast([128, NC, 32]),
                                                ALU.mult), a, ss)
                a = V(lambda e: e.tensor_tensor(nd[:, :, :], nd[:, :, :], X[:, :, :], ALU.add), a)
                x2 = layernorm(nd, nd2, X, a)

        layer1()
        Q.meet()

        def layer2():
            with ExitStack() as ph:
                lasts = sb(ph, "lasts", [128, NC], I32)
                firsts = sb(ph, "firsts", [128, NC])
                feqs = sb(ph, "feqs", [128, 1], I32)
                pes = sb(ph, "pes", [128, 4])
                cTs = sb(ph, "cTs", [64, 128])
                wTs = sb(ph, "wTs", [64, 128])
                with ExitStack() as ph2:
                    pos = sb(ph2, "poss", [128, J], I32)
                    ranked = rank("b", U["src"], known["seg"], cs, firsts, pos)
                    Q.meet()
                    with ExitStack() as ph3:
                        ki = sb(ph3, "ki2", [128, J], I32)
                        p4 = sb(ph3, "p4", [128, J, 4], I32)
                        a2 = sb(ph3, "a2b", [128, J, 2])
                        load(ki[:, :], U["dst"][:, 0].rearrange("(p j) -> p j", p=128), "r1")
                        l = load(a2[:, :, :], U["a2"].rearrange("(p j) f -> p j f", p=128), "r1")
                        V(lambda e: e.tensor_copy(p4[:, :, 0], srcs[:, :]))
                        V(lambda e: e.tensor_copy(p4[:, :, 1], ki[:, :]), l)
                        a = V(lambda e: e.tensor_copy(p4[:, :, 2:4].bitcast(F32), a2[:, :, :]), l)
                        for j in range(J):
                            sc = scatter(T4, pos[:, j:j + 1], p4[:, j, :], f"s4{j // 784}", a, ranked)
                            if j == 783:
                                sc0 = sc
                Q.meet()
                ks = sb(ph, "m01s", [128, J])
                gi = sb(ph, "gi", [128, J], I32)
                wt = sb(ph, "wt", [128, J, 4])
                w2s = sb(ph, "w2s", [32, 16, 4, 32])
                rt = sb(ph, "rt", [32, 32])
                bb = sb(ph, "bb", [128, 32])
                w2v = w2.rearrange("(b a) i o -> i b a o", a=5)
                for b1 in range(4):
                    for a1 in range(4):
                        for c in range(4):
                            load(w2s[:, 4 * b1 + a1, c, :], w2v[:, b1 + c // 2, a1 + c % 2, :], "w2")
                load(rt[:, :], root2, "w2")
                wl = load(bb[:, :], bias2.rearrange("(o f) -> o f", o=1).to_broadcast([128, 32]), "w2")
                with ExitStack() as ph2:
                    t4 = sb(ph2, "t4", [128, J, 4], I32)
                    kf = sb(ph2, "kf2", [128, J])
                    ta = sb(ph2, "ta", [128, J])
                    tb = sb(ph2, "tb", [128, J])
                    ti = sb(ph2, "ti", [128, J], I32)
                    fr = sb(ph2, "fr", [128, 2, J])
                    pli = sb(ph2, "pli2", [128, 1], I32)
                    plf = sb(ph2, "plf2", [128, 1])
                    z = V(lambda e: e.memset(pli[:, :], -1))
                    l = load(t4[:, :, :], T4.rearrange("(p j) f -> p j f", p=128), "r2", sc, sc0)
                    l = load(pli[1:128, :], T4.rearrange("(p j) f -> p j f", p=128)[0:127, J - 1, 0:1], "r2", z)
                    a = V(lambda e: e.tensor_copy(kf[:, :], t4[:, :, 0]), l)
                    b = V(lambda e: e.tensor_copy(plf[:, :], pli[:, :]), l)
                    c = V(None, a, b)
                    sg2 = segments("sb", kf, plf, c, ks, None, cs, firsts, lasts, None, pes, feqs, cTs, wTs)
                    a = None
                    acc = V(lambda e: e.tensor_scalar(gi[:, :], t4[:, :, 1], 16.0, None, ALU.mult), l, c)
                    for d in range(2):
                        f = fr[:, d, :]
                        a = V(lambda e, d=d: e.tensor_scalar(tb[:, :], t4[:, :, 2 + d].bitcast(F32), 4.0, 0.0,
                                                             ALU.mult, ALU.max), l, a, acc)
                        a = V(lambda e: e.tensor_scalar(tb[:, :], tb[:, :], 4.0, None, ALU.min), a)
                        a = V(lambda e: e.tensor_copy(ti[:, :], tb[:, :]), a)
                        a = V(lambda e: e.tensor_copy(ta[:, :], ti[:, :]), a)
                        a = V(lambda e, f=f: e.tensor_tensor(f, ta[:, :], tb[:, :], ALU.is_gt), a)
                        a = V(lambda e, f=f: e.tensor_tensor(ta[:, :], ta[:, :], f, ALU.subtract), a)
                        a = V(lambda e: e.tensor_scalar(ta[:, :], ta[:, :], 3.0, None, ALU.min), a)
                        b = V(lambda e, f=f: e.tensor_tensor(f, tb[:, :], ta[:, :], ALU.subtract), a)
                        acc = V(lambda e, d=d: e.scalar_tensor_tensor(out=gi[:, :], in0=ta[:, :], scalar=[1.0, 4.0][d],
                                                                      in1=gi[:, :], op0=ALU.mult, op1=ALU.add), a, acc)
                        a = V(None, b, acc)
                    b = V(lambda e: e.tensor_tensor(wt[:, :, 3], fr[:, 0, :], fr[:, 1, :], ALU.mult), a)
                    n1 = V(lambda e: e.tensor_scalar(ta[:, :], fr[:, 0, :], -1.0, 1.0, ALU.mult, ALU.add), a)
                    n2 = V(lambda e: e.tensor_scalar(tb[:, :], fr[:, 1, :], -1.0, 1.0, ALU.mult, ALU.add), a)
                    V(lambda e: e.tensor_tensor(wt[:, :, 0], ta[:, :], tb[:, :], ALU.mult), n1, n2)
                    V(lambda e: e.tensor_tensor(wt[:, :, 1], fr[:, 0, :], tb[:, :], ALU.mult), n2)
                    wts_ok = V(lambda e: e.tensor_tensor(wt[:, :, 2], ta[:, :], fr[:, 1, :], ALU.mult), n1)
                Q.meet()
                with ExitStack() as ph2:
                    XT = sb(ph2, "xt2", [32, NC * 128])
                    Yb = [sb(ph2, f"yb{i}", [128, 2048]) for i in range(2)]
                    ev = {}
                    for c in range(NC):
                        t = T(lambda e, c=c: e.transpose(ps[c % 2][0:32, 0:128], X[:, c, :], ident[:, :]),
                              ev.get(c - 2))
                        ev[c] = V(lambda e, c=c: e.tensor_copy(XT[:, c * 128:(c + 1) * 128], ps[c % 2][0:32, 0:128]), t)
                    ys, ye = {}, {}
                    for c in range(NC):
                        for k in range(4):
                            t = T(lambda e, c=c, k=k: e.matmul(
                                ps[2 + k][:, 0:512], XT[:, c * 128:(c + 1) * 128],
                                w2s[:, 4 * k:4 * k + 4, :, :].rearrange("i a b o -> i (a b o)"), start=True, stop=True),
                                ev[c], wl, ye.get((c - 1, k)))
                            w = V if k % 2 else S
                            ye[(c, k)] = w(lambda e, c=c, k=k: (e.tensor_copy if k % 2 else e.copy)(
                                Yb[c % 2][:, 512 * k:512 * k + 512], ps[2 + k][:, 0:512]), t, ys.get(c - 2))
                        ys[c] = load(Y.rearrange("(p c k) f -> p c (k f)", p=128, c=NC)[:, c, :], Yb[c % 2][:, :],
                                     f"y{c % 2}", ye[(c, 2)], ye[(c, 3)])
                        t = T(lambda e, c=c: e.matmul(ps[6][:, (c % 16) * 32:(c % 16) * 32 + 32],
                                                      XT[:, c * 128:(c + 1) * 128], rt[:, :], start=True, stop=True),
                              ye.get("r"))
                        if c % 16 == 15 or c == NC - 1:
                            n = c % 16 + 1
                            ye["r"] = V(lambda e, c=c, n=n: e.tensor_copy(
                                nd2[:, c - n + 1:c + 1, :], ps[6][:, 0:32 * n].rearrange("p (a b) -> p a b", b=32)), t)
                    ydone = [ys[NC - 1], ys[NC - 2]]
                Q.meet()
                Gb = [sb(ph, f"l2g{i}", [128, C, 4, 32]) for i in range(2)]
                Pb = sb(ph, "l2p", [128, C, 4, 32])
                Vb = sb(ph, "l2v", [128, C, 32])
                O = [sb(ph, f"l2o{i}", [128, C, 32]) for i in range(2)]
                prod, scd, stq = [None] * NCH, [None] * NCH, [None] * NCH
                for c in range(NCH):
                    s = c % 2
                    for j in range(C):
                        g = gather(Gb[s][:, j, :, :].rearrange("p a b -> p (a b)"), Y, gi[:, c * C + j:c * C + j + 1],
                                   f"l2g{s}", prod[c - 2] if c >= 2 else None, *ydone)
                    prod[c] = V(lambda e, c=c, s=s: e.tensor_tensor(
                        Pb[:, :, :, :], Gb[s][:, :, :, :],
                        wt[:, c * C:(c + 1) * C, :, None].to_broadcast([128, C, 4, 32]), ALU.mult), g,
                        scd[c - 1] if c else None)
                    a = V(lambda e: e.tensor_tensor(Pb[:, :, 0:2, :], Pb[:, :, 0:2, :], Pb[:, :, 2:4, :], ALU.add), prod[c])
                    a = V(lambda e: e.tensor_tensor(Vb[:, :, :], Pb[:, :, 0, :], Pb[:, :, 1, :], ALU.add), a)
                    scd[c] = scans(lambda f, s=s: O[s][:, :, f], ks[:, c * C:(c + 1) * C], lambda f: Vb[:, :, f],
                                   (lambda f: 0.0) if c == 0 else (lambda f, s=s: O[1 - s][:, C - 1, f:f + 1]),
                                   32, ALU.mult, ALU.add, a, stq[c - 2] if c >= 2 else None,
                                   scd[c - 1] if c else None)
                    stq[c] = load(W2[0:NE, :].rearrange("(p j) f -> p j f", p=128)[:, c * C:(c + 1) * C, :],
                                  O[s][:, :, :], f"l2s{s}", scd[c])
                fx = fixup_sum("f2", O[(NCH - 1) % 2][:, C - 1, :], 32, [(0, 32, False)], W2, feqs, cTs, wTs,
                               stq[-2:], scd[-1])
                ng = node_gather(nd, W2, lasts, "ng", fx)
                a = V(lambda e: e.tensor_scalar(st[:, 0, :], cs[:, :], 1.0, None, ALU.max))
                a = V(lambda e: e.reciprocal(st[:, 0, :], st[:, 0, :]), a)
                a = V(lambda e: e.tensor_tensor(nd[:, :, :], nd[:, :, :], st[:, 0, :, None].to_broadcast([128, NC, 32]),
                                                ALU.mult), a, ng)
                a = V(lambda e: e.tensor_tensor(nd[:, :, :], nd[:, :, :], nd2[:, :, :], ALU.add), a)
                a = V(lambda e: e.tensor_tensor(nd[:, :, :], nd[:, :, :], bb[:, None, :].to_broadcast([128, NC, 32]),
                                                ALU.add), a)
                a = V(lambda e: e.tensor_tensor(nd[:, :, :], nd[:, :, :], X[:, :, :], ALU.add), a)
                x3 = layernorm(nd, nd2, X, a)

        layer2()
        Q.meet()

        def layer3():
            with ExitStack() as ph:
                XC = sb(ph, "xc", [128, NC, 32])
                PN = sb(ph, "pn", [128, NC, 32])
                QN = sb(ph, "qn", [128, NC, 32])
                XT = sb(ph, "xt3", [32, NC * 128])
                Zb = sb(ph, "z3", [128, NC, 64])
                Zc = [sb(ph, f"zc{i}", [128, 128]) for i in range(2)]
                ZT = [sb(ph, f"zt{i}", [128, 128]) for i in range(2)]
                rc = sb(ph, "rc", [128, NC])
                has = sb(ph, "has", [128, NC])
                BPQ = sb(ph, "bpq", [32, 5, 64])
                PC = sb(ph, "pc", [8, 5, 32])
                EWT = sb(ph, "ewt", [8, 5, 128])
                EB = sb(ph, "ebc", [8, 5])
                PB = sb(ph, "pbc", [128, 5, 32])
                WR = sb(ph, "wr", [128, 5, 8, 32])
                bm = sb(ph, "bm", [128, 8])
                C0 = sb(ph, "c0", [128, 5, 32])
                BO = sb(ph, "bo", [32, 5, 4, 32])
                LW = sb(ph, "lw", [32, 5, 32])
                LB_ = sb(ph, "lbb", [128, 5, 32])
                POB = sb(ph, "pobc", [32, 5])
                AO = sb(ph, "ao", [128, 5, 32])
                CO = sb(ph, "co", [128, 5, 32])
                z1 = V(lambda e: e.memset(BPQ[:, :, :], 0.0))
                z2 = V(lambda e: e.memset(BO[:, :, :, :], 0.0))
                z3 = G(lambda e: e.memset(bm[:, :], 1.0))
                z3 = G(lambda e: e.affine_select(out=bm[:, :], in_=bm[:, :], compare_op=ALU.is_ge, fill=0.0, base=0,
                                                 pattern=[[-16, 8]], channel_multiplier=1), z3)
                z3 = G(lambda e: e.affine_select(out=bm[:, :], in_=bm[:, :], compare_op=ALU.is_ge, fill=0.0, base=15,
                                                 pattern=[[16, 8]], channel_multiplier=-1), z3)
                for l in range(5):
                    for t in range(4):
                        r8 = slice(8 * t, 8 * t + 8)
                        load(BPQ[r8, l, 8 * t:8 * t + 8], pW[l, t, 0:8, :], "w3", z1, z2)
                        load(BPQ[r8, l, 32 + 8 * t:40 + 8 * t], pW[l, t, 8:16, :], "w3")
                        load(PC[:, l, 8 * t:8 * t + 8], pW[l, t, 16:24, :], "w3")
                        for i in range(4):
                            load(BO[r8, l, i, 8 * t:8 * t + 8], poW[l, t, 8 * i:8 * i + 8, :].rearrange("k f -> f k"),
                                 "w3")
                    for j in range(8):
                        load(EWT[:, l, 16 * j:16 * j + 16], eW[l].rearrange("a b -> b a"), "w3")
                    load(EB[:, l:l + 1], eb[l].rearrange("(a b) -> a b", b=1), "w3")
                    load(PB[:, l, :], pb[l].rearrange("(o t) f -> o (t f)", o=1).to_broadcast([128, 32]), "w3")
                    load(LW[:, l, :], lW[l], "w3")
                    load(LB_[:, l, :], lb[l].rearrange("(o f) -> o f", o=1).to_broadcast([128, 32]), "w3")
                    wl = load(POB[:, l:l + 1], pob[l].rearrange("t (f o) -> (t f) o", o=1), "w3")
                pv = [None] * 4
                for l in range(5):
                    t1 = T(lambda e, l=l: e.matmul(ps[0][:, 0:32], EWT[:, l, :], PC[:, l, :], start=True, stop=True),
                           wl, pv[0])
                    pv[0] = V(lambda e, l=l: e.tensor_tensor(
                        WR[:, l, :, :], ps[0][:, None, 0:32].to_broadcast([128, 8, 32]),
                        bm[:, :, None].to_broadcast([128, 8, 32]), ALU.mult), t1, z3)
                    t1 = T(lambda e, l=l: e.matmul(ps[1][:, 0:32], EB[:, l:l + 1].to_broadcast([8, 128]), PC[:, l, :],
                                                   start=True, stop=True), wl, pv[1])
                    pv[1] = V(lambda e, l=l: e.tensor_tensor(C0[:, l, :], ps[1][:, 0:32], PB[:, l, :], ALU.add), t1)
                    t1 = T(lambda e, l=l: e.matmul(ps[2][:, 0:32], BO[:, l, :, :].rearrange("a b c -> a (b c)"),
                                                   LW[:, l, :], start=True, stop=True), wl, pv[2])
                    pv[2] = V(lambda e, l=l: e.tensor_copy(AO[:, l, :], ps[2][:, 0:32]), t1)
                    t1 = T(lambda e, l=l: e.matmul(ps[3][:, 0:32], POB[:, l:l + 1].to_broadcast([32, 128]), LW[:, l, :],
                                                   start=True, stop=True), wl, pv[3])
                    pv[3] = V(lambda e, l=l: e.tensor_tensor(CO[:, l, :], ps[3][:, 0:32], LB_[:, l, :], ALU.add), t1)
                weights = V(None, *pv)
                a = V(lambda e: e.tensor_scalar(rc[:, :], cnt[:, :], 1.0, None, ALU.max))
                V(lambda e: e.reciprocal(rc[:, :], rc[:, :]), a)
                V(lambda e: e.tensor_scalar(has[:, :], cnt[:, :], 0.0, None, ALU.is_gt))
                xcr = V(lambda e: e.tensor_copy(XC[:, :, :], X[:, :, :]))
                Gb = [sb(ph, f"l3g{i}", [128, C, 32]) for i in range(2)]
                Ea = [sb(ph, f"l3e{i}", [128, C * 16]) for i in range(2)]
                ET = [sb(ph, f"l3t{i}", [128, 7, 128]) for i in range(1)]
                Vb = sb(ph, "l3v", [128, C, 32])
                O = [sb(ph, f"l3o{i}", [128, C, 64]) for i in range(2)]
                Q.meet()
                x_ready, qprev = None, None
                for l in range(5):
                    ev = {}
                    for c in range(NC):
                        t = T(lambda e, c=c: e.transpose(ps[c % 2][0:32, 0:128], XC[:, c, :], ident[:, :]),
                              ev.get(c - 2), x_ready)
                        ev[c] = V(lambda e, c=c: e.tensor_copy(XT[:, c * 128:(c + 1) * 128], ps[c % 2][0:32, 0:128]), t)
                    pq = {}
                    for c in range(NC):
                        o = (c % 8) * 64
                        t = T(lambda e, c=c, o=o, l=l: e.matmul(ps[2 + (c // 8) % 2][:, o:o + 64],
                                                                XT[:, c * 128:(c + 1) * 128], BPQ[:, l, :],
                                                                start=True, stop=True), ev[c], pq.get(c // 8 - 2))
                        if c % 8 == 7 or c == NC - 1:
                            n, k = c % 8 + 1, c // 8
                            pv = ps[2 + k % 2][:, 0:64 * n].rearrange("p (a b) -> p a b", b=64)
                            V(lambda e, c=c, n=n, pv=pv: e.tensor_copy(PN[:, c - n + 1:c + 1, :], pv[:, :, 0:32]), t)
                            pq[k] = V(lambda e, c=c, n=n, pv=pv, l=l: e.tensor_tensor(
                                QN[:, c - n + 1:c + 1, :], pv[:, :, 32:64],
                                C0[:, l, None, :].to_broadcast([128, n, 32]), ALU.add), t, qprev)
                    qprev = load(node_view(TQ), QN[:, :, :], "tq", pq[NC // 8])
                    addd, scd, stq, evr, et = [None] * NCH, [None] * NCH, [None] * NCH, {}, [None] * NCH
                    for c in range(NCH):
                        s = c % 2
                        for j in range(C):
                            g = gather(Gb[s][:, j, :], TQ, srcs[:, c * C + j:c * C + j + 1], f"l3g{s}",
                                       addd[c - 2] if c >= 2 else None, qprev)
                        ld = load(Ea[s][:, :], U["a16"].rearrange("(p j) f -> p (j f)", p=128)[
                            :, c * C * 16:(c + 1) * C * 16], f"l3e{s}", et[c - 2] if c >= 2 else None)
                        for k in range(7):
                            b = 4 + k % 2
                            t = T(lambda e, k=k, s=s, b=b: e.transpose(ps[b][:, 0:128], Ea[s][:, 128 * k:128 * k + 128],
                                                                       ident[:, :]), ld, evr.get(("t", b)))
                            evr[("t", b)] = S(lambda e, k=k, b=b: e.copy(ET[0][:, k, :], ps[b][:, 0:128]), t,
                                              evr.get(("m", k)))
                            et[c] = t
                            h = 6 + (k // 2) % 2
                            t = T(lambda e, k=k, l=l, h=h: e.matmul(
                                ps[h][:, 256 * (k % 2):256 * (k % 2) + 256], ET[0][:, k, :],
                                WR[:, l, :, :].rearrange("p a b -> p (a b)"), start=True, stop=True),
                                evr[("t", b)], evr.get(("a", h)))
                            evr[("m", k)] = t
                            if k % 2 == 1 or k == 6:
                                n = 8 * (k % 2 + 1)
                                j0 = 8 * (k - k % 2)
                                addd[c] = V(lambda e, s=s, h=h, n=n, j0=j0: e.tensor_tensor(
                                    Vb[:, j0:j0 + n, :], Gb[s][:, j0:j0 + n, :],
                                    ps[h][:, 0:32 * n].rearrange("p (a b) -> p a b", b=32), ALU.add), g, t,
                                    scd[c - 1] if c else None)
                                evr[("a", h)] = addd[c]
                        scd[c] = scans(lambda f, s=s: O[s][:, :, f], m01[:, c * C:(c + 1) * C], lambda f: Vb[:, :, f],
                                       (lambda f: 0.0) if c == 0 else (lambda f, s=s: O[1 - s][:, C - 1, f:f + 1]),
                                       32, ALU.mult, ALU.add, addd[c], stq[c - 2] if c >= 2 else None,
                                       scd[c - 1] if c else None)
                        scd[c] = scans(lambda f, s=s: O[s][:, :, 32 + f], mneg[:, c * C:(c + 1) * C],
                                       lambda f: Vb[:, :, f],
                                       (lambda f: -BIG) if c == 0 else (
                                           lambda f, s=s: O[1 - s][:, C - 1, 32 + f:33 + f]),
                                       32, ALU.add, ALU.max)
                        stq[c] = load(W3[0:NE, :].rearrange("(p j) f -> p j f", p=128)[:, c * C:(c + 1) * C, :],
                                      O[s][:, :, :], f"l3s{s}", scd[c])
                    fx = fixup_sum(f"f3{l}", O[(NCH - 1) % 2][:, C - 1, :], 64, [(0, 32, False), (32, 64, True)], W3,
                                   feq, contT, wT, stq[-2:], scd[-1])
                    ng = node_gather(Zb, W3, lastq, "ng", fx)
                    a = V(lambda e: e.tensor_tensor(nd[:, :, :], PN[:, :, :], cnt[:, :, None].to_broadcast([128, NC, 32]),
                                                    ALU.mult), pq[NC // 8])
                    a = V(lambda e: e.tensor_tensor(Zb[:, :, 0:32], Zb[:, :, 0:32], nd[:, :, :], ALU.add), a, ng)
                    b = V(lambda e: e.tensor_tensor(Zb[:, :, 32:64], Zb[:, :, 32:64], PN[:, :, :], ALU.add), ng)
                    b = V(lambda e: e.tensor_tensor(Zb[:, :, 32:64], Zb[:, :, 32:64],
                                                    has[:, :, None].to_broadcast([128, NC, 32]), ALU.mult), b)
                    zz = V(None, a, b)
                    zt, zc, mm = {}, {}, {}
                    for c in range(NC):
                        s = c % 2
                        V(lambda e, c=c, s=s: e.tensor_copy(Zc[s][:, 0:32], XC[:, c, :]), zt.get(c - 2), zz)
                        V(lambda e, c=c, s=s: e.tensor_scalar(Zc[s][:, 32:64], Zb[:, c, 0:32], rc[:, c:c + 1], None,
                                                              ALU.mult))
                        a = V(lambda e, c=c, s=s: e.tensor_copy(Zc[s][:, 64:128], Zb[:, c, :]))
                        zt[c] = T(lambda e, s=s: e.transpose(ps[s][:, 0:128], Zc[s][:, :], ident[:, :]), a,
                                  zc.get(c - 2))
                        zc[c] = S(lambda e, s=s: e.copy(ZT[s][:, :], ps[s][:, 0:128]), zt[c], mm.get(c - 2))
                        mm[c] = T(lambda e, s=s, l=l: e.matmul(ps[2 + s][:, 0:32], ZT[s][:, :], AO[:, l, :], start=True,
                                                               stop=True), zc[c], evr.get(("o", s)))
                        evr[("o", s)] = V(lambda e, c=c, s=s, l=l: e.tensor_tensor(
                            nd2[:, c, :], ps[2 + s][:, 0:32], CO[:, l, :], ALU.add), mm[c], x_ready)
                    a = V(None, evr[("o", 0)], evr[("o", 1)])
                    x_ready = V(lambda e: e.tensor_scalar(XC[:, :, :], nd2[:, :, :], 0.0, None, ALU.max), a, mm[NC - 1])
                    Q.step()
                a = V(lambda e: e.tensor_tensor(nd[:, :, :], XC[:, :, :], X[:, :, :], ALU.add), x_ready)
                y = layernorm(nd, nd2, X, a)
                for p0, p1 in ((0, 112), (112, 127)):
                    o = load(out[NC * p0:NC * p1, :].rearrange("(p c) f -> p c f", c=NC), X[p0:p1, :, :], "out", y)
                n = NN - 127 * NC
                o = load(out[127 * NC:NN, :].rearrange("(o c) f -> o c f", o=1), X[127:128, 0:n, :], "out", y)
                Q.q["sync"].append((None, (o,), None, None))

        layer3()
        Q.emit()


_INS = ["x", "src", "dst", "edge_attr_16", "edge_attr_2", "edge_attr_32", "L0_gnn_eps", "L1_gnn_beta",
        "L2_gnn_weight", "L2_gnn_root_weight", "L2_gnn_bias", "L3_gnn_edge_W", "L3_gnn_edge_b", "L3_gnn_pre_W",
        "L3_gnn_pre_b", "L3_gnn_post_W", "L3_gnn_post_b", "L3_gnn_lin_W", "L3_gnn_lin_b"]


def kernel(**inputs):
    import numpy as _np
    import concourse.bacc as _bacc
    from concourse.bass_utils import run_bass_kernel_spmd as _run

    nc = _bacc.Bacc("TRN2", target_bir_lowering=False, num_devices=1)
    arrays, args = {}, []
    for name in _INS:
        a = _np.ascontiguousarray(inputs[name])
        arrays[f"in_{name}"] = a
        args.append(nc.dram_tensor(f"in_{name}", a.shape, mybir.dt.from_np(a.dtype), kind="ExternalInput").ap())
    out = nc.dram_tensor("out_0", (NN, 32), F32, kind="ExternalOutput").ap()
    program(nc, *args, out)
    r = _run(nc, [arrays], core_ids=[0])
    return r.results[0]["out_0"]
```

```python
from contextlib import ExitStack

import concourse.bass as bass
from concourse import mybir

F32 = mybir.dt.float32
I32 = mybir.dt.int32
BF16 = mybir.dt.bfloat16
ALU = mybir.AluOpType
ACT = mybir.ActivationFunctionType
AXX = mybir.AxisListType.X

NN = 6250
NC = 49
NP = 128 * NC
E = 200000
J = 1568
NE = 128 * J
C = 56
NCH = J // C
H = 14
NG = J // H
GR = 7
KP = 13
BIG = 3.0e38
ENG = ("sync", "scalar", "vector", "tensor", "gpsimd")


class Done:

    def __init__(self, eng, phase):
        self.eng, self.phase, self.used, self.value = eng, phase, False, None


class Chan:

    def __init__(self, sem):
        self.sem, self.n = sem, 0


class Queues:

    def __init__(self, nc, ctx):
        self.nc, self.ctx = nc, ctx
        self.q = {e: [] for e in ENG}
        self.phase = 0
        self.chans = {}
        self.met = set()

    def chan(self, name):
        if name not in self.chans:
            self.chans[name] = Chan(self.ctx.enter_context(self.nc.semaphore("d_" + name)))
        return self.chans[name]

    def do(self, eng, fn, *after):
        d = Done(eng, self.phase)
        self._after(after)
        self.q[eng].append((fn, after, d, None))
        return d

    def dma(self, eng, fn, ch, *after):
        ch = self.chan(ch)
        ch.n += 16
        self._after(after)
        self.q[eng].append((fn, after, None, ch))
        return (ch, ch.n)

    def _after(self, after):
        for a in after:
            if isinstance(a, Done):
                a.used = True

    def branch(self, flag):
        self.meet()
        for e in ENG:
            self.q[e].append(("if", flag, None, None))

    def join(self, *dmas):
        self.meet(*dmas)
        for e in ENG:
            self.q[e].append(("join", None, None, None))

    def step(self):
        self.phase += 1

    def meet(self, *dmas):
        last = []
        for e in ENG:
            real = [d for fn, _, d, _ in self.q[e] if callable(fn) and d is not None]
            if real and real[-1] not in self.met:
                real[-1].used = True
                last.append(real[-1])
                self.met.add(real[-1])
        for e in ENG:
            self.q[e].append((None, tuple(last) + dmas, None, None))
        self.step()

    def emit(self):
        sems, count = {}, {}
        for e in ENG:
            for fn, after, d, ch in self.q[e]:
                if d is not None and d.used:
                    key = (e, d.phase)
                    if key not in sems:
                        sems[key] = self.ctx.enter_context(self.nc.semaphore(f"e_{e}_{d.phase}"))
                    count[key] = count.get(key, 0) + 1
                    d.value = count[key]
        block = self.ctx.enter_context(self.nc.Block())
        for e in ENG:
            engine_block = {"sync": block.sync, "scalar": block.scalar, "vector": block.vector,
                             "tensor": block.tensor, "gpsimd": block.gpsimd}[e]

            def body(eng, e=e):
                seen, before, inner = {}, None, None
                for fn, after, d, ch in self.q[e]:
                    if fn == "if":
                        before = dict(seen)
                        inner = eng.If(eng.value_load(after, min_val=0, max_val=1) != 0)
                        inner.__enter__()
                        continue
                    if fn == "join":
                        inner.__exit__(None, None, None)
                        seen = before
                        continue
                    need = {}
                    for a in after:
                        if a is None:
                            continue
                        if isinstance(a, Done):
                            key, sem, v = (a.eng, a.phase), sems[(a.eng, a.phase)], a.value
                        else:
                            key, sem, v = id(a[0]), a[0].sem, a[1]
                        if v > need.get(key, (None, 0))[1]:
                            need[key] = (sem, v)
                    for key, (sem, v) in need.items():
                        if v > seen.get(key, 0):
                            eng.wait_ge(sem, v)
                            seen[key] = v
                    if fn is None:
                        if d is not None and d.used:
                            eng.sem_inc(sems[(e, d.phase)], 1)
                        continue
                    ins = fn(eng)
                    if ch is not None:
                        ins.then_inc(ch.sem, 16)
                    elif d.used:
                        ins.then_inc(sems[(e, d.phase)], 1)

            engine_block(body)


def program(nc, x, src, dst, ea16, ea2, ea32, eps, beta, w2, root2, bias2,
            eW, eb, pW, pb, poW, pob, lW, lb, out):
    ctx = ExitStack()
    with ctx:
        ctx.enter_context(nc.allow_non_contiguous_dma(reason="small weights, flags and index rows"))
        Q = Queues(nc, ctx)

        def V(fn, *after):
            return Q.do("vector", fn, *after)

        def S(fn, *after):
            return Q.do("scalar", fn, *after)

        def T(fn, *after):
            return Q.do("tensor", fn, *after)

        def G(fn, *after):
            return Q.do("gpsimd", fn, *after)

        def load(o, i, ch, *after, eng="sync"):
            return Q.dma(eng, lambda e: e.dma_start(o, i), ch, *after)

        def gather(o, table, idx, ch, *after):
            return Q.dma("gpsimd", lambda e: e.indirect_dma_start(
                o, None, table, bass.IndirectOffsetOnAxis(ap=idx, axis=0)), ch, *after)

        def scatter(table, idx, i, ch, *after):
            return Q.dma("gpsimd", lambda e: e.indirect_dma_start(
                table, bass.IndirectOffsetOnAxis(ap=idx, axis=0), i, None), ch, *after)

        def dram(name, shape, dt=F32):
            return nc.dram_tensor(name, shape, dt, kind="Internal").ap()

        def sb(st, name, shape, dt=F32):
            return st.enter_context(nc.sbuf_tensor(name, shape, dt))

        U = {"src": dram("U_src", [NE, 1], I32), "dst": dram("U_dst", [NE, 1], I32),
             "a2": dram("U_a2", [NE, 2]), "a16": dram("U_a16", [NE, 16]), "a32": dram("U_a32", [NE, 32])}
        R = dram("R", [NE, 52])
        KT = dram("KT", [J, 128], BF16)
        T0 = dram("T0", [NP, 32])
        T1 = dram("T1", [NP, 33])
        NH = dram("NH", [NP, 32])
        Y = dram("Y", [NP * 16, 128])
        TQ = dram("TQ", [NP, 32])
        S0 = dram("S0", [NE + NP, 32])
        T4 = dram("T4", [NE, 4], I32)
        W0 = dram("W0", [NE + 16, 32])
        W1 = dram("W1", [NE + 16, 34])
        W2 = dram("W2", [NE + 16, 32])
        W3 = dram("W3", [NE + 16, 64])

        ps = [ctx.enter_context(nc.psum_tensor(f"ps{i}", [128, 512], F32)) for i in range(8)]

        ident = sb(ctx, "ident", [128, 128])
        slt = sb(ctx, "slt", [128, 128])
        trib = sb(ctx, "trib", [128, 128], BF16)
        iot = sb(ctx, "iot", [128, 128], BF16)
        ioti = sb(ctx, "ioti", [128, 128], I32)
        iotp = sb(ctx, "iotp", [128, 1])
        iotpi = sb(ctx, "iotpi", [128, 1], I32)
        nodei = sb(ctx, "nodei", [128, NC], I32)
        nodef = sb(ctx, "nodef", [128, NC])
        zer = sb(ctx, "zer", [128, 1024])
        padi = sb(ctx, "padi", [64, 11], I32)
        X = sb(ctx, "X", [128, NC, 32])
        cnt = sb(ctx, "cnt", [128, NC])
        first = sb(ctx, "first", [128, NC])
        lastq = sb(ctx, "lastq", [128, NC], I32)
        startq = sb(ctx, "startq", [128, NC], I32)
        srcs = sb(ctx, "srcs", [128, J], I32)
        m01 = sb(ctx, "m01", [128, J])
        mneg = sb(ctx, "mneg", [128, J])
        pe = sb(ctx, "pe", [128, 4])
        feq = sb(ctx, "feq", [128, 1], I32)
        k0i = sb(ctx, "k0i", [128, 1], I32)
        cs = sb(ctx, "cnts", [128, NC])
        contT = sb(ctx, "contT", [64, 128])
        wT = sb(ctx, "wT", [64, 128])
        bcol = sb(ctx, "bcol", [128, 2])
        nd = sb(ctx, "nd", [128, NC, 32])
        nd2 = sb(ctx, "nd2", [128, NC, 32])
        st = sb(ctx, "st", [128, 4, NC])
        flag = sb(ctx, "flag", [1, 1], I32)

        g0 = G(lambda e: e.memset(ident[:, :], 0.0))
        g1 = G(lambda e: e.affine_select(out=ident[:, :], in_=ident[:, :], compare_op=ALU.not_equal,
                                         fill=1.0, base=0, pattern=[[-1, 128]], channel_multiplier=1), g0)
        g2 = G(lambda e: e.memset(slt[:, :], 1.0), g1)
        g3 = G(lambda e: e.affine_select(out=slt[:, :], in_=slt[:, :], compare_op=ALU.is_gt,
                                         fill=0.0, base=0, pattern=[[1, 128]], channel_multiplier=-1), g2)
        g4 = G(lambda e: e.iota(ioti[:, :], [[1, 128]], base=0, channel_multiplier=0), g3)
        g5 = G(lambda e: e.iota(iotpi[:, :], [[0, 1]], base=0, channel_multiplier=1), g4)
        g6 = G(lambda e: e.iota(nodei[:, :], [[1, NC]], base=0, channel_multiplier=NC), g5)
        g7 = G(lambda e: e.memset(padi[:, :], NP - 1), g6)
        g8 = G(lambda e: e.memset(zer[:, :], 0.0), g7)
        V(lambda e: e.tensor_copy(trib[:, :], slt[:, :]), g3)
        V(lambda e: e.tensor_copy(iot[:, :], ioti[:, :]), g4)
        V(lambda e: e.tensor_copy(iotp[:, :], iotpi[:, :]), g5)
        V(lambda e: e.tensor_copy(nodef[:, :], nodei[:, :]), g6)

        def padded(k, a, fill, ready, n):
            d = U[k].rearrange("e f -> (e f)")
            f = U[k].shape[1]
            load(d[0:E * f].rearrange("(a b) -> a b", a=n), a, "c" + k)
            return load(d[E * f:NE * f].rearrange("(a b) -> a b", a=64), fill, "c" + k, ready)

        in_dst = padded("dst", dst.rearrange("(a b) -> a b", a=16), padi[:, :], g7, 16)
        in_src = padded("src", src.rearrange("(a b) -> a b", a=16), padi[:, :], g7, 16)
        load(T0[0:NN, :].rearrange("(a b) f -> a (b f)", a=125), x.rearrange("(a b) f -> a (b f)", a=125), "ct")
        load(bcol[:, 0:1], eps.rearrange("(a b) -> a b", a=1).to_broadcast([128, 1]), "ct")
        load(bcol[:, 1:2], beta.rearrange("(a b) -> a b", a=1).to_broadcast([128, 1]), "ct")
        in_x = load(T0[NN:NP, :], zer[0:22, 0:32], "ct", g8)
        in_32 = padded("a32", ea32.rearrange("(a b) f -> a (b f)", a=64), zer[0:64, 0:352], g8, 64)
        in_16 = padded("a16", ea16.rearrange("(a b) f -> a (b f)", a=64), zer[0:64, 0:176], g8, 64)
        in_2 = padded("a2", ea2.rearrange("(a b) f -> a (b f)", a=64), zer[0:64, 0:22], g8, 64)
        for w in (W0, W1, W2, W3):
            no_edge = load(w[NE:NE + 16, :], zer[0:16, 0:w.shape[1]], "cw", g8)
        S0v = S0[0:NE, :].rearrange("(p j) f -> p (j f)", p=128)
        for k in range(NE * 32 // 128 // 1024):
            starts_zeroed = load(S0v[:, k * 1024:(k + 1) * 1024], zer[:, :], "zs", g8, eng="scalar")

        def in_order():
            with ExitStack() as ph:
                ki = sb(ph, "oki", [128, J], I32)
                pl = sb(ph, "opl", [128, 1], I32)
                kf = sb(ph, "okf", [128, J])
                pf = sb(ph, "opf", [128, 1])
                vi = sb(ph, "ovi", [128, J])
                vs = sb(ph, "ovs", [128, 2])
                keys = U["dst"][:, 0].rearrange("(p j) -> p j", p=128)
                z = V(lambda e: e.memset(pl[:, :], -1))
                load(ki[:, :], keys, "ok", in_dst)
                l = load(pl[1:128, :], keys[0:127, J - 1:J], "ok", z)
                a = V(lambda e: e.tensor_copy(kf[:, :], ki[:, :]), l)
                b = V(lambda e: e.tensor_copy(pf[:, :], pl[:, :]), l)
                c = V(lambda e: e.tensor_tensor(vi[:, 1:J], kf[:, 1:J], kf[:, 0:J - 1], ALU.is_lt), a)
                d = V(lambda e: e.tensor_tensor(vi[:, 0:1], kf[:, 0:1], pf[:, :], ALU.is_lt), a, b)
                c = V(lambda e: e.tensor_reduce(vs[:, 0:1], vi[:, :], AXX, ALU.add), c, d)
                o = V(lambda e: e.memset(vs[:, 1:2], 1.0))
                t = T(lambda e: e.matmul(ps[0][0:1, 0:1], vs[:, 0:1], vs[:, 1:2], start=True, stop=True), c, o)
                V(lambda e: e.tensor_scalar(flag[:, :], ps[0][0:1, 0:1], 1.0, None, ALU.min), t)

        in_order()

        def split_key(Kf, rk, ti, ready, lo, lob, hib):
            a = V(lambda e: e.tensor_scalar(ti[:, :], Kf[:, :], 1.0 / 49, 0.5 / 49, ALU.mult, ALU.add), ready)
            a = V(lambda e: e.tensor_copy(lo[:, :], ti[:, :]), a)
            a = V(lambda e: e.scalar_tensor_tensor(out=rk[:, :], in0=lo[:, :], scalar=-49.0, in1=Kf[:, :],
                                                   op0=ALU.mult, op1=ALU.add), a)
            a = V(lambda e: e.tensor_scalar(Kf[:, :], rk[:, :], 0.0, None, ALU.is_lt), a)
            b = V(lambda e: e.tensor_tensor(lo[:, :], lo[:, :], Kf[:, :], ALU.subtract), a)
            c = V(lambda e: e.scalar_tensor_tensor(out=hib[:, :], in0=Kf[:, :], scalar=49.0, in1=rk[:, :],
                                                   op0=ALU.mult, op1=ALU.add), b)
            return V(lambda e: e.tensor_copy(lob[:, :], lo[:, :]), b, c)

        def turn_rows(tag, lo, ready):
            with ExitStack() as st_:
                ktb = [sb(st_, tag + f"ktb{i}", [128, 128], BF16) for i in range(2)]
                wr, cp = [None, None], []
                for i in range(13):
                    w = min(128, J - 128 * i)
                    t = T(lambda e, i=i, w=w: e.transpose(ps[i % 2][0:w, 0:128], lo[:, 128 * i:128 * i + w],
                                                          ident[:, :]), ready, cp[i - 2] if i >= 2 else None)
                    cp.append(S(lambda e, i=i, w=w: e.copy(ktb[i % 2][0:w, :], ps[i % 2][0:w, 0:128]), t, wr[i % 2]))
                    wr[i % 2] = load(KT[128 * i:128 * i + w, :], ktb[i % 2][0:w, :], tag + f"kt{i % 2}", cp[-1])
                return wr

        class Ones:

            def __init__(self, st_, tag, full):
                self.AL = [sb(st_, tag + f"AL{i}", [128, H, 128], BF16) for i in range(2)]
                self.AH = [sb(st_, tag + f"AH{i}", [128, H, NC], BF16) for i in range(2)]
                self.ex = sb(st_, tag + "ex", [128, NC + 1])
                self.rs = sb(st_, tag + "rs", [128, 2])
                if full:
                    self.AT = [sb(st_, tag + f"AT{i}", [128, H, 128]) for i in range(2)]
                    self.EQ = sb(st_, tag + "EQ", [128, H, 128], BF16)
                    self.M1 = [sb(st_, tag + f"M1{i}", [128, H, 128], BF16) for i in range(2)]
                    self.LB = [sb(st_, tag + f"LB{i}", [128, H, 128], BF16) for i in range(2)]
                    self.Cs = [sb(st_, tag + f"Cs{i}", [128, NC]) for i in range(2)]
                    self.pr = sb(st_, tag + "pr", [128, 7, NC])
                self.used = [None, None]

        def one_hots(B, g, lob, hib, ready):
            s = g % 2
            h0 = V(lambda e: e.tensor_tensor(
                B.AH[s][:, :, :], iot[:, None, 0:NC].to_broadcast([128, H, NC]),
                hib[:, g * H:(g + 1) * H, None].to_broadcast([128, H, NC]), ALU.is_equal), ready, B.used[s])
            h1 = V(lambda e: e.tensor_tensor(
                B.AL[s][:, :, :], iot[:, None, :].to_broadcast([128, H, 128]),
                lob[:, g * H:(g + 1) * H, None].to_broadcast([128, H, 128]), ALU.is_equal), B.used[s])
            return h0, h1

        def histogram(B, lob, hib, ready, cnt_t, first_t, got, bank, bank2):
            for g in range(NG):
                s = g % 2
                _, h = one_hots(B, g, lob, hib, ready)
                for j in range(H):
                    B.used[s] = T(lambda e, g=g, s=s, j=j: e.matmul(
                        ps[bank][:, 0:NC], B.AL[s][:, j, :], B.AH[s][:, j, :], start=(g == 0 and j == 0),
                        stop=(g == NG - 1 and j == H - 1)), h)
                if g < NG - 1:
                    yield
            c = V(lambda e: e.tensor_copy(cnt_t[:, :], ps[bank][:, 0:NC]), B.used[(NG - 1) % 2])
            got["bank"] = c
            z = V(lambda e: e.memset(B.ex[:, :], 0.0))
            a = V(lambda e: e.tensor_tensor_scan(B.ex[:, 1:NC + 1], cnt_t[:, :], cnt_t[:, :], 0.0,
                                                 ALU.add, ALU.bypass), c, z)
            t = T(lambda e: e.matmul(ps[bank2][:, 0:1], slt[:, :], B.ex[:, NC:NC + 1], start=True, stop=True), a)
            a = V(lambda e: e.tensor_copy(B.rs[:, 0:1], ps[bank2][:, 0:1]), t)
            got["first"] = V(lambda e: e.tensor_scalar(first_t[:, :], B.ex[:, 0:NC], B.rs[:, 0:1], None, ALU.add), a)
            yield

        def places(B, tag, lob, hib, first_t, kt_out, pos, got, bank, lbanks):
            hist = T(lambda e: e.matmul(ps[bank][:, 0:NC], ident[:, :], first_t[:, :], start=True, stop=False,
                                        skip_group_check=True), got["first"], got["bank"])
            lbd, red, csr, rd, h4 = [None, None], {}, [None, None], None, None

            def sums(g, lk):
                nonlocal rd
                s = g % 2
                for k in range(2):
                    b = lbanks[2 * s + k]
                    pd = V(lambda e, b=b, k=k: e.tensor_tensor(
                        B.pr[:, :, :], ps[b][:, 0:7 * NC].rearrange("p (a b) -> p a b", a=7),
                        B.AH[s][:, 7 * k:7 * k + 7, :], ALU.mult), lk, rd)

                    def add(e, k=k):
                        with nc.allow_low_precision(reason="integers under 2**24"):
                            return e.tensor_reduce(pos[:, g * H + 7 * k:g * H + 7 * k + 7], B.pr[:, :, :], AXX, ALU.add)

                    rd = V(add, pd)
                    red[b] = rd
                B.used[s] = rd

            late = None
            for g in range(NG):
                s = g % 2
                ld = load(B.LB[s][:, :, :], KT[g * H:(g + 1) * H, :].rearrange("(o j) p -> o j p", o=1)
                          .to_broadcast([128, H, 128]), tag + f"lb{s}", lbd[s], *kt_out)
                h0, h1 = one_hots(B, g, lob, hib, None)
                h2 = V(lambda e, s=s: e.tensor_scalar(B.AT[s][:, :, :], B.LB[s][:, :, :], iotp[:, 0:1], None,
                                                      ALU.is_equal), ld, B.used[s])
                h3 = V(lambda e, g=g, s=s: e.tensor_tensor(
                    B.EQ[:, :, :], B.LB[s][:, :, :],
                    lob[:, g * H:(g + 1) * H, None].to_broadcast([128, H, 128]), ALU.is_equal), ld, h4)
                lbd[s] = h3
                h4 = V(lambda e, s=s: e.tensor_tensor(B.M1[s][:, :, :], B.EQ[:, :, :],
                                                      trib[:, None, :].to_broadcast([128, H, 128]), ALU.mult),
                       h3, B.used[s])
                if late is not None:
                    sums(*late)
                for j in range(H):
                    i = g * H + j
                    b = lbanks[2 * s + j // 7]
                    o = NC * (j % 7)
                    cp = S(lambda e, i=i: e.copy(B.Cs[i % 2][:, :], ps[bank][:, 0:NC]), hist, csr[i % 2])
                    hist = T(lambda e, s=s, j=j: e.matmul(
                        ps[bank][:, 0:NC], B.AL[s][:, j, :], B.AH[s][:, j, :], start=False, stop=False,
                        skip_group_check=True), h1, h0, cp)
                    csr[i % 2] = T(lambda e, s=s, j=j, i=i, b=b, o=o: e.matmul(
                        ps[b][:, o:o + NC], B.AT[s][:, j, :], B.Cs[i % 2][:, :], start=True, stop=False,
                        skip_group_check=True), cp, h2, red.get(b))
                    lk = T(lambda e, s=s, j=j, b=b, o=o: e.matmul(
                        ps[b][:, o:o + NC], B.M1[s][:, j, :], B.AH[s][:, j, :], start=False, stop=True,
                        skip_group_check=True), h4, h0)
                late = (g, lk)
                yield
            sums(*late)
            got["placed"] = rd

        known = {}

        def sort_by_dst():
            with ExitStack() as ph:
                pos = sb(ph, "posd", [128, J], I32)
                with ExitStack() as ph2:
                    Ki = sb(ph2, "aKi", [128, J], I32)
                    lo = sb(ph2, "alo", [128, J])
                    lob = sb(ph2, "alob", [128, J], BF16)
                    hib = sb(ph2, "ahib", [128, J], BF16)
                    B = Ones(ph2, "a", True)
                    kin = load(Ki[:, :], U["dst"][:, 0].rearrange("(p j) -> p j", p=128), "aki", in_dst, in_src,
                               in_2, in_16, in_32)
                    Kf = sb(ph2, "aKf", [128, J])
                    rk = sb(ph2, "ark", [128, J])
                    rdy = V(lambda e: e.tensor_copy(Kf[:, :], Ki[:, :]), kin)
                    rdy = split_key(Kf, rk, Ki, rdy, lo, lob, hib)
                    rows = turn_rows("a", lo, rdy)
                    got = {}
                    for _ in histogram(B, lob, hib, rdy, cnt, first, got, 2, 6):
                        pass
                    for _ in places(B, "a", lob, hib, first, rows, pos, got, 2, (4, 5, 0, 1)):
                        pass
                    ranked = got["placed"]
                Q.meet()
                with ExitStack() as ph2:
                    pay = [sb(ph2, f"pay{i}", [128, C, 52]) for i in range(2)]
                    b32 = [sb(ph2, f"b32_{i}", [128, C, 32]) for i in range(2)]
                    b16 = [sb(ph2, f"b16_{i}", [128, C, 16]) for i in range(2)]
                    bsm = [sb(ph2, f"bsm_{i}", [128, C, 4]) for i in range(2)]
                    bi = [sb(ph2, f"bi_{i}", [128, 2, C], I32) for i in range(2)]
                    sc = [None, None]
                    cpd = [None, None]
                    for c in range(NCH):
                        s = c % 2
                        v = {k: U[k].rearrange("(p j) f -> p j f", p=128)[:, c * C:(c + 1) * C, :] for k in U}
                        load(b32[s][:, :, :], v["a32"], f"pl{s}", cpd[s])
                        load(b16[s][:, :, :], v["a16"], f"pl{s}")
                        load(bsm[s][:, :, 0:2], v["a2"], f"pl{s}")
                        load(bi[s][:, 0, :], v["src"].rearrange("p j f -> p (j f)"), f"pl{s}")
                        l = load(bi[s][:, 1, :], v["dst"].rearrange("p j f -> p (j f)"), f"pl{s}")
                        a = V(lambda e, s=s: e.tensor_copy(pay[s][:, :, 0:32], b32[s][:, :, :]), l, sc[s])
                        a = V(lambda e, s=s: e.tensor_copy(pay[s][:, :, 32:48], b16[s][:, :, :]), l)
                        a = V(lambda e, s=s: e.tensor_copy(pay[s][:, :, 48:50], bsm[s][:, :, 0:2]), l)
                        a = V(lambda e, s=s: e.tensor_copy(pay[s][:, :, 50:52].bitcast(I32),
                                                           bi[s][:, :, :].rearrange("p k j -> p j k")), l)
                        cpd[s] = a
                        for j in range(C):
                            sc[s] = scatter(R, pos[:, c * C + j:c * C + j + 1], pay[s][:, j, :], f"sc{s}", a, ranked)
                    scattered = sc
                Q.meet()
                with ExitStack() as ph2:
                    pay_o = [sb(ph2, f"qay{i}", [128, C, 52]) for i in range(2)]
                    b32_o = [sb(ph2, f"c32_{i}", [128, C, 32]) for i in range(2)]
                    b16_o = [sb(ph2, f"c16_{i}", [128, C, 16]) for i in range(2)]
                    b2 = [sb(ph2, f"c2_{i}", [128, C, 2]) for i in range(2)]
                    bi_o = [sb(ph2, f"ci_{i}", [128, 2, C], I32) for i in range(2)]
                    stq = [None, None]
                    cpd = [None, None]
                    for c in range(NCH):
                        s = c % 2
                        v = {k: U[k].rearrange("(p j) f -> p j f", p=128)[:, c * C:(c + 1) * C, :] for k in U}
                        l = load(pay_o[s][:, :, :], R.rearrange("(p j) f -> p j f", p=128)[:, c * C:(c + 1) * C, :],
                                 f"ql{s}", cpd[s], *scattered)
                        V(lambda e, s=s: e.tensor_copy(b32_o[s][:, :, :], pay_o[s][:, :, 0:32]), l, stq[s])
                        V(lambda e, s=s: e.tensor_copy(b16_o[s][:, :, :], pay_o[s][:, :, 32:48]), l)
                        V(lambda e, s=s: e.tensor_copy(b2[s][:, :, :], pay_o[s][:, :, 48:50]), l)
                        a = V(lambda e, s=s: e.tensor_copy(bi_o[s][:, :, :].rearrange("p k j -> p j k"),
                                                           pay_o[s][:, :, 50:52].bitcast(I32)), l)
                        cpd[s] = a
                        load(v["a32"], b32_o[s][:, :, :], f"qs{s}", a)
                        load(v["a16"], b16_o[s][:, :, :], f"qs{s}")
                        load(v["a2"], b2[s][:, :, :], f"qs{s}")
                        load(v["src"].rearrange("p j f -> p (j f)"), bi_o[s][:, 0, :], f"qs{s}")
                        stq[s] = load(v["dst"].rearrange("p j f -> p (j f)"), bi_o[s][:, 1, :], f"qs{s}")
                    known["sorted_in"] = stq

        Q.branch(flag[0:1, 0:1])
        sort_by_dst()
        Q.join(*known["sorted_in"])

        def segments(tag, key_f, prev_last, ready, m01_t, mneg_t, pe_t, feq_t, cT, wTt, q, fl):
            a = V(lambda e: e.memset(m01_t[:, 0:1], 0.0))
            a = V(lambda e: e.tensor_tensor(m01_t[:, 1:J], key_f[:, 1:J], key_f[:, 0:J - 1], ALU.is_equal), a, ready)
            masks = a
            if mneg_t is not None:
                masks = V(lambda e: e.tensor_scalar(mneg_t[:, :], m01_t[:, :], -1.0, BIG, ALU.add, ALU.mult), a)
            a = V(lambda e: e.tensor_scalar(q[:, :], key_f[:, :], key_f[:, 0:1], None, ALU.is_equal), ready)
            a = V(lambda e: e.tensor_reduce(fl[:, 0:1], q[:, :], AXX, ALU.add), a)
            b = V(lambda e: e.scalar_tensor_tensor(out=fl[:, 1:2], in0=iotp[:, 0:1], scalar=float(J),
                                                   in1=fl[:, 0:1], op0=ALU.mult, op1=ALU.add), a)
            b = V(lambda e: e.tensor_scalar(feq_t[:, :], fl[:, 1:2], -1.0, None, ALU.add), b)
            c = V(lambda e: e.tensor_tensor(pe_t[:, 0:1], key_f[:, 0:1], prev_last[:, 0:1], ALU.is_equal), ready)
            d = V(lambda e: e.tensor_scalar(fl[:, 2:3], fl[:, 0:1], float(J), None, ALU.is_ge), a)
            c = V(lambda e: e.tensor_tensor(pe_t[:, 1:2], pe_t[:, 0:1], fl[:, 2:3], ALU.mult), c, d)
            t1 = T(lambda e: e.matmul(ps[6][0:64, 0:128], pe_t[:, 0:1].to_broadcast([128, 64]), ident[:, :],
                                      start=True, stop=True), c)
            t2 = T(lambda e: e.matmul(ps[7][0:64, 0:128], pe_t[:, 1:2].to_broadcast([128, 64]), ident[:, :],
                                      start=True, stop=True), c)
            V(lambda e: e.tensor_copy(cT[:, :], ps[6][0:64, 0:128]), t1)
            d = V(lambda e: e.tensor_copy(wTt[:, :], ps[7][0:64, 0:128]), t2)
            return masks, V(None, masks, b, d)

        def node_places(cnt_t, first_t, last_t, start_t, ready):
            nf, nf2 = st[:, 0, :], st[:, 1, :]
            h = V(lambda e: e.tensor_scalar(nf, cnt_t[:, :], 0.0, None, ALU.is_gt), ready)
            i = V(lambda e: e.tensor_tensor(nf2, first_t[:, :], cnt_t[:, :], ALU.add), ready)
            i = V(lambda e: e.tensor_scalar(nf2, nf2, -1.0 - NE, None, ALU.add), i)
            i = V(lambda e: e.tensor_tensor(nf2, nf2, nf, ALU.mult), h, i)
            i = V(lambda e: e.tensor_scalar(last_t[:, :], nf2, float(NE), None, ALU.add), i)
            if start_t is not None:
                i = V(lambda e: e.tensor_tensor(nf2, first_t[:, :], nodef[:, :], ALU.subtract), i)
                i = V(lambda e: e.tensor_scalar(nf2, nf2, -float(NE), None, ALU.add), i)
                i = V(lambda e: e.tensor_tensor(nf2, nf2, nf, ALU.mult), i)
                i = V(lambda e: e.tensor_tensor(nf2, nf2, nodef[:, :], ALU.add), i)
                i = V(lambda e: e.tensor_scalar(start_t[:, :], nf2, float(NE), None, ALU.add), i)
            return i

        stb = sb(ctx, "stb", [128, 4, NC])
        firsts = sb(ctx, "firsts", [128, NC])
        segf = sb(ctx, "segf", [128, 4])
        RX = sb(ctx, "RX", [128, NC, 32])
        BPQ = sb(ctx, "bpq", [32, 5, 64])
        WR = sb(ctx, "wr", [128, 5, 8, 32])
        C0 = sb(ctx, "c0", [128, 5, 32])
        AO = sb(ctx, "ao", [128, 5, 32])
        CO = sb(ctx, "co", [128, 5, 32])
        rc = sb(ctx, "rc", [128, NC])
        has = sb(ctx, "has", [128, NC])
        early, bgs, l0 = ExitStack(), ExitStack(), ExitStack()
        p4 = sb(early, "p4", [128, J, 4], I32)
        poss = sb(early, "poss", [128, J], I32)
        lobs = sb(bgs, "lobs", [128, J], BF16)
        hibs = sb(bgs, "hibs", [128, J], BF16)
        B = Ones(bgs, "b", True)
        lobd = sb(l0, "lobd", [128, J], BF16)
        hibd = sb(l0, "hibd", [128, J], BF16)
        BD = Ones(l0, "bd", False)
        G0 = [sb(l0, f"l0g{i}", [128, C, 32]) for i in range(2)]
        bg, bgd = {}, {}

        def dst_segments():
            with ExitStack() as ph:
                ki = sb(ph, "ki", [128, J], I32)
                kf = sb(ph, "kf", [128, J])
                lo = sb(ph, "klo", [128, J])
                q = sb(ph, "kq", [128, J])
                pli = sb(ph, "pli", [128, 1], I32)
                plf = sb(ph, "plf", [128, 1])
                keyflat = U["dst"][:, 0]
                z = V(lambda e: e.memset(pli[:, :], -1))
                load(ki[:, :], keyflat.rearrange("(p j) -> p j", p=128), "k1", in_dst)
                l = load(pli[1:128, :], keyflat.rearrange("(p j) -> p j", p=128)[0:127, J - 1:J], "k1", z)
                a = V(lambda e: e.tensor_copy(kf[:, :], ki[:, :]), l)
                b = V(lambda e: e.tensor_copy(plf[:, :], pli[:, :]), l)
                V(lambda e: e.tensor_copy(k0i[:, :], ki[:, 0:1]), l)
                c = V(None, a, b)
                _, known["seg"] = segments("sa", kf, plf, c, m01, mneg, pe, feq, contT, wT, q, segf)
                a = split_key(kf, q, ki, known["seg"], lo, lobd, hibd)
                a = V(lambda e: e.tensor_copy(kf[:, :], srcs[:, :]), a, known["srcs"])
                known["split_s"] = split_key(kf, q, ki, a, lo, lobs, hibs)
                known["rows"] = turn_rows("ks", lo, known["split_s"])

        def rank_src():
            yield from histogram(B, lobs, hibs, known["split_s"], cs, firsts, bg, 2, 6)
            yield from places(B, "b", lobs, hibs, firsts, known["rows"], poss, bg, 2, (4, 5, 0, 1))

        def count_dst():
            yield from histogram(BD, lobd, hibd, known["split_s"], cnt, first, bgd, 3, 7)
            bgd["dst"] = node_places(cnt, first, lastq, startq, bgd["first"])

        def scans(o, data0, data1, init, width, op0, op1, *after):
            last = None
            for f in range(width):
                ini = init(f)
                last = V(lambda e, f=f, ini=ini: e.tensor_tensor_scan(o(f), data0, data1(f), ini, op0, op1), *after)
            return last

        def layernorm(y, o, c0, c1, *after):
            n = c1 - c0
            mu, var = st[:, 0, c0:c1], st[:, 1, c0:c1]
            yv, sq, ov = y[:, c0:c1, :], nd2[:, c0:c1, :], o[:, c0:c1, :]
            a = V(lambda e: e.tensor_reduce(mu, yv, AXX, ALU.add), *after)
            a = V(lambda e: e.tensor_scalar(mu, mu, 1.0 / 32, None, ALU.mult), a)
            a = V(lambda e: e.tensor_tensor(yv, yv, mu[:, :, None].to_broadcast([128, n, 32]), ALU.subtract), a)
            b = V(lambda e: e.tensor_tensor(sq, yv, yv, ALU.mult), a)
            b = V(lambda e: e.tensor_reduce(var, sq, AXX, ALU.add), b)
            b = V(lambda e: e.tensor_scalar(var, var, 1.0 / 32, 1e-5, ALU.mult, ALU.add), b)
            c = S(lambda e: e.activation(var, var, ACT.Sqrt), b)
            c = V(lambda e: e.reciprocal(var, var), c)
            return V(lambda e: e.tensor_tensor(ov, yv, var[:, :, None].to_broadcast([128, n, 32]), ALU.mult), c)

        def node_view(t):
            return t.rearrange("(p c) f -> p c f", p=128)

        def node_gather(o, table, idx, tag, *after):
            got = []
            for c in range(NC):
                t = gather(o[:, c, :], table, idx[:, c:c + 1], f"{tag}{c // GR}", *after)
                if c % GR == GR - 1:
                    got.append(t)
            return got

        def chunks(n, tail=()):
            out_, j = [], 0
            while j < J - sum(tail):
                out_.append((j, n))
                j += n
            for n in tail:
                out_.append((j, n))
                j += n
            assert j == J
            return out_

        def slots(t, j0, n):
            return t[0:NE, :].rearrange("(p j) f -> p j f", p=128)[:, j0:j0 + n, :]

        def fixup(tag, lastcol, width, kind, table, feq_t, cT, wTt, stored, ready):
            with ExitStack() as st_:
                eT = sb(st_, tag + "eT", [64, 128])
                sT = sb(st_, tag + "sT", [64, 128])
                cTr = sb(st_, tag + "cT", [64, 128])
                wn = sb(st_, tag + "wn", [64, 128])
                cn = sb(st_, tag + "cn", [64, 128])
                row = sb(st_, tag + "row", [128, 64])
                row2 = sb(st_, tag + "row2", [128, 64])
                g = gather(row[:, 0:width], table, feq_t[:, 0:1], "fx", *stored)
                t = T(lambda e: e.transpose(ps[6][0:width, 0:128], lastcol, ident[:, :]), ready)
                b = V(lambda e: e.tensor_scalar(wn[:, :], wTt[:, :], -1.0, BIG, ALU.add, ALU.mult), ready)
                b = V(lambda e: e.tensor_scalar(cn[:, :], cT[:, :], -1.0, BIG, ALU.add, ALU.mult), b)
                m = V(lambda e: e.memset(cTr[:, :], 0.0), b)
                a = V(lambda e: e.tensor_copy(eT[0:width, :], ps[6][0:width, 0:128]), t)
                c = None
                for f0, f1, mx in kind:
                    if mx:
                        m = V(lambda e, f0=f0, f1=f1: e.memset(cTr[f0:f1, 0:1], -BIG), m)
                    d0 = wn if mx else wTt
                    c = V(lambda e, f0=f0, f1=f1, d0=d0, mx=mx: e.tensor_tensor_scan(
                        sT[f0:f1, :], d0[f0:f1, :], eT[f0:f1, :], -BIG if mx else 0.0,
                        ALU.add if mx else ALU.mult, ALU.max if mx else ALU.add), a, b)
                    c = V(lambda e, f0=f0, f1=f1, mx=mx: e.tensor_tensor(
                        cTr[f0:f1, 1:128], sT[f0:f1, 0:127], (cn if mx else cT)[f0:f1, 1:128],
                        ALU.add if mx else ALU.mult), c, m)
                t = T(lambda e: e.transpose(ps[7][:, 0:width], cTr[0:width, :], ident[0:width, 0:width]), c, m)
                for f0, f1, mx in kind:
                    c = V(lambda e, f0=f0, f1=f1, mx=mx: e.tensor_tensor(
                        row2[:, f0:f1], row[:, f0:f1], ps[7][:, f0:f1], ALU.max if mx else ALU.add), t, g)
                return scatter(table, feq_t[:, 0:1], row2[:, 0:width], "fx", c)

        def gather0(c, ready):
            for j in range(C):
                g = gather(G0[c % 2][:, j, :], T0, srcs[:, c * C + j:c * C + j + 1], f"l0g{c % 2}", ready, in_x)
            return g

        def layer0():
            with ExitStack() as ph:
                Ea = [sb(ph, f"l0e{i}", [128, C, 32]) for i in range(2)]
                O = [sb(ph, f"l0o{i}", [128, C, 32]) for i in range(2)]
                Gb = G0
                CH = chunks(C)
                N = len(CH)
                scd, stq = [None] * N, [None] * N
                for c, (j0, n) in enumerate(CH):
                    s = c % 2
                    g = gather0(c, scd[c - 2]) if c >= 2 else known[("g0", c)]
                    l = load(Ea[s][:, 0:n, :], slots(U["a32"], j0, n), f"l0e{s}",
                             scd[c - 2] if c >= 2 else in_32)
                    if c < 7:
                        for _ in range(16):
                            next(src_work)
                    else:
                        for k in range(6):
                            next(dst_work, None)
                            if k < 4:
                                next(src_work, None)
                    a = V(lambda e, s=s, n=n: e.tensor_tensor(Gb[s][:, 0:n, :], Gb[s][:, 0:n, :], Ea[s][:, 0:n, :],
                                                              ALU.add), g, l)
                    a = S(lambda e, s=s, n=n: e.activation(Gb[s][:, 0:n, :], Gb[s][:, 0:n, :], ACT.Relu), a)
                    scd[c] = scans(lambda f, s=s, n=n: O[s][:, 0:n, f], m01[:, j0:j0 + n],
                                   lambda f, s=s, n=n: Gb[s][:, 0:n, f],
                                   (lambda f: 0.0) if c == 0 else
                                   (lambda f, s=s, k=CH[c - 1][1]: O[1 - s][:, k - 1, f:f + 1]),
                                   32, ALU.mult, ALU.add, a, stq[c - 2] if c >= 2 else None,
                                   scd[c - 1] if c else None)
                    stq[c] = load(slots(W0, j0, n), O[s][:, 0:n, :], f"l0s{s}", scd[c])
                for _ in dst_work:
                    pass
                fx = fixup("f0", O[(N - 1) % 2][:, CH[-1][1] - 1, :], 32, [(0, 32, False)], W0, feq, contT, wT,
                           (stq[-2], stq[-1], no_edge), scd[-1])
                ng = node_gather(nd, W0, lastq, "ng", fx, bgd["dst"])
                tw = V(lambda e: e.tensor_scalar(stb[:, 2, 0:1], bcol[:, 0:1], 2.0, None, ALU.add), in_x, known["X"])
                for g in range(NC // GR):
                    c0, c1 = GR * g, GR * g + GR
                    a = V(lambda e, c0=c0, c1=c1: e.scalar_tensor_tensor(
                        out=nd[:, c0:c1, :], in0=X[:, c0:c1, :], scalar=stb[:, 2, 0:1], in1=nd[:, c0:c1, :],
                        op0=ALU.mult, op1=ALU.add), tw, ng[g])
                    layernorm(nd, X, c0, c1, a)
            Q.meet()

        def layer1():
            C1 = C // 2
            with ExitStack() as ph:
                NB = sb(ph, "l1n", [128, NC, 34])
                Gb = [sb(ph, f"l1g{i}", [128, C1, 33]) for i in range(3)]
                Sb = [sb(ph, f"l1s{i}", [128, C1, 32]) for i in range(2)]
                Db = [sb(ph, f"l1d{i}", [128, C1, 32]) for i in range(2)]
                Pb = sb(ph, "l1p", [128, C1, 33])
                O = [sb(ph, f"l1o{i}", [128, C1, 34]) for i in range(2)]
                K0 = sb(ph, "l1k0", [128, 32])
                M = sb(ph, "l1m", [128, J + 1])
                ev = sb(ph, "l1e", [128, C1])
                av = sb(ph, "l1a", [128, 2, C1])
                fe = sb(ph, "l1fe", [33, 8, 128])
                row = sb(ph, "l1row", [128, 34])
                row2 = sb(ph, "l1row2", [128, 34])
                fs = sb(ph, "l1fs", [128, 8])
                cl = [sb(ph, f"cl{i}", [128, 98], I32 if i > 3 else F32) for i in range(6)]
                cla = sb(ph, "cla", [128, 98, 2])
                a = V(lambda e: e.tensor_tensor(nd[:, :, :], X[:, :, :], X[:, :, :], ALU.mult))
                a = V(lambda e: e.tensor_reduce(st[:, 0, :], nd[:, :, :], AXX, ALU.add), a)
                a = S(lambda e: e.activation(st[:, 0, :], st[:, 0, :], ACT.Sqrt), a)
                a = V(lambda e: e.tensor_scalar(st[:, 0, :], st[:, 0, :], 1e-12, None, ALU.max), a)
                a = V(lambda e: e.reciprocal(st[:, 1, :], st[:, 0, :]), a)
                b = V(lambda e: e.tensor_copy(NB[:, :, 32], st[:, 1, :]), a)
                c_ = V(lambda e: e.tensor_copy(NB[:, :, 0:32], X[:, :, :]))
                d = load(node_view(T1), NB[:, :, 0:33], "t1", b, c_)
                a = V(lambda e: e.tensor_scalar(st[:, 2, :], st[:, 1, :], bcol[:, 1:2], None, ALU.mult), a)
                a = V(lambda e: e.tensor_tensor(nd[:, :, :], X[:, :, :],
                                                st[:, 2, :, None].to_broadcast([128, NC, 32]), ALU.mult), a)
                dh = load(node_view(NH), nd[:, :, :], "t2", a)
                mi = V(lambda e: e.memset(M[:, 0:1], -BIG))
                CH = chunks(C1)
                N = len(CH)
                prod, fil, scd, stq, dd = [None] * N, [None] * N, [None] * N, [None] * N, [None] * N
                ld = {}

                def cells(k):
                    j0 = 98 * k
                    tb, ta, f, acc, ti, kd = (t[:, :] for t in cl)
                    load(kd, U["dst"][:, 0].rearrange("(p j) -> p j", p=128)[:, j0:j0 + 98], "cl", bg.get("cl"))
                    l = load(cla[:, :, :], slots(U["a2"], j0, 98), "cl", in_2)
                    V(lambda e: e.tensor_copy(p4[:, j0:j0 + 98, 0], srcs[:, j0:j0 + 98]))
                    a = V(lambda e: e.tensor_scalar(acc, kd, 16.0, None, ALU.mult), l, bg.get("cl"))
                    for d in range(2):
                        a = V(lambda e, d=d: e.tensor_scalar(tb, cla[:, :, d], 4.0, 0.0, ALU.mult, ALU.max), a)
                        a = V(lambda e: e.tensor_scalar(tb, tb, 4.0, None, ALU.min), a)
                        a = V(lambda e: e.tensor_copy(ti, tb), a)
                        a = V(lambda e: e.tensor_copy(ta, ti), a)
                        a = V(lambda e: e.tensor_tensor(f, ta, tb, ALU.is_gt), a)
                        a = V(lambda e: e.tensor_tensor(ta, ta, f, ALU.subtract), a)
                        a = V(lambda e: e.tensor_scalar(ta, ta, 3.0, None, ALU.min), a)
                        b = V(lambda e, d=d: e.tensor_tensor(p4[:, j0:j0 + 98, 2 + d].bitcast(F32), tb, ta,
                                                             ALU.subtract), a)
                        a = V(lambda e, d=d: e.scalar_tensor_tensor(out=acc, in0=ta, scalar=[1.0, 4.0][d], in1=acc,
                                                                    op0=ALU.mult, op1=ALU.add), a, b)
                    bg["cl"] = V(lambda e: e.tensor_copy(p4[:, j0:j0 + 98, 1], acc), a)

                for c, (j0, n) in enumerate(CH):
                    s, s3 = c % 2, c % 3
                    for j in range(n):
                        g = gather(Gb[s3][:, j, :], T1, srcs[:, j0 + j:j0 + j + 1], f"l1g{s3}", d,
                                   prod[c - 3] if c >= 3 else None)
                    if c == 1:
                        k0 = gather(K0[:, :], NH, k0i[:, 0:1], "k0g", dh)
                        for k in range(NC):
                            ld["ss"] = scatter(S0, startq[:, k:k + 1], nd[:, k, :], "ss", a_nd, starts_zeroed)
                    if c == 0:
                        a_nd = a

                    def fill_and_dot(c, s, s3, j0, n, g):
                        if c % 2:
                            next(src_work, None)
                        l = load(Sb[s][:, 0:n, :], slots(S0, j0, n), f"l1s{s}", fil[c - 2] if c >= 2 else None,
                                 ld["ss"])
                        if c == 0:
                            l = V(lambda e: e.tensor_copy(Sb[0][:, 0, :], K0[:, :]), l, k0)
                        fil[c] = scans(lambda f: Db[s][:, 0:n, f], m01[:, j0:j0 + n], lambda f: Sb[s][:, 0:n, f],
                                       (lambda f: 0.0) if c == 0 else (lambda f: Db[1 - s][:, C1 - 1, f:f + 1]),
                                       32, ALU.mult, ALU.add, l, dd[c - 1] if c else None,
                                       fil[c - 1] if c else None)
                        a = V(lambda e: e.tensor_tensor(Pb[:, 0:n, 0:32], Gb[s3][:, 0:n, 0:32], Db[s][:, 0:n, :],
                                                        ALU.mult), g, fil[c], scd[c - 1] if c else None)
                        dd[c] = a
                        a = V(lambda e: e.tensor_reduce(ev[:, 0:n], Pb[:, 0:n, 0:32], AXX, ALU.add), a)
                        a = V(lambda e: e.tensor_tensor(ev[:, 0:n], ev[:, 0:n], Gb[s3][:, 0:n, 32], ALU.mult), a)
                        a = V(lambda e: e.tensor_tensor_scan(M[:, 1 + j0:1 + j0 + n], mneg[:, j0:j0 + n],
                                                             ev[:, 0:n], M[:, j0:j0 + 1], ALU.add, ALU.max), a, mi)
                        b = V(lambda e: e.tensor_tensor(ev[:, 0:n], ev[:, 0:n], M[:, 1 + j0:1 + j0 + n],
                                                        ALU.subtract), a)
                        m = V(lambda e: e.tensor_tensor(av[:, 0, 0:n], M[:, j0:j0 + n], M[:, 1 + j0:1 + j0 + n],
                                                        ALU.subtract), a)
                        m = V(lambda e: e.tensor_scalar(av[:, 0, 0:n], av[:, 0, 0:n], 0.0, None, ALU.min), m)
                        b = S(lambda e: e.activation(ev[:, 0:n], ev[:, 0:n], ACT.Exp), b)
                        m = S(lambda e: e.activation(av[:, 0, 0:n], av[:, 0, 0:n], ACT.Exp), m)
                        m2 = V(lambda e: e.tensor_copy(O[s][:, 0:n, 33], M[:, 1 + j0:1 + j0 + n]), a,
                               stq[c - 2] if c >= 2 else None)
                        m = V(lambda e: e.tensor_tensor(av[:, 1, 0:n], av[:, 0, 0:n], m01[:, j0:j0 + n],
                                                        ALU.mult), m)
                        q = V(lambda e: e.tensor_tensor(Pb[:, 0:n, 0:32], Gb[s3][:, 0:n, 0:32],
                                                        ev[:, 0:n, None].to_broadcast([128, n, 32]), ALU.mult), b)
                        prod[c] = q
                        q = V(lambda e: e.tensor_copy(Pb[:, 0:n, 32], ev[:, 0:n]), q)
                        scd[c] = scans(lambda f: O[s][:, 0:n, f], av[:, 1, 0:n], lambda f: Pb[:, 0:n, f],
                                       (lambda f: 0.0) if c == 0 else (lambda f: O[1 - s][:, C1 - 1, f:f + 1]),
                                       33, ALU.mult, ALU.add, q, m, m2, scd[c - 1] if c else None)
                        stq[c] = load(slots(W1, j0, n), O[s][:, 0:n, :], f"l1o{s}", scd[c])

                    if c == 0:
                        first_args = (c, s, s3, j0, n, g)
                    else:
                        if c == 1:
                            fill_and_dot(*first_args)
                        fill_and_dot(c, s, s3, j0, n, g)
                    if c % 3 == 2 and c // 3 < 16:
                        cells(c // 3)
                OL = O[(N - 1) % 2]
                for _ in src_work:
                    pass

                def send(j0, j1):
                    for j in range(j0, j1):
                        t = scatter(T4, poss[:, j:j + 1], p4[:, j, :], f"s4{j // 784}", bg["cl"], bg["placed"])
                        known[f"s4{j // 784}"] = t

                send(0, 40)
                g = gather(row[:, :], W1, feq[:, 0:1], "fx", stq[-1], stq[-2], no_edge)
                send(40, 60)
                t1 = T(lambda e: e.transpose(ps[6][0:33, 0:128], OL[:, C1 - 1, 0:33], ident[:, :]), scd[-1])
                t2 = T(lambda e: e.matmul(ps[7][0:33, 0:128], OL[:, C1 - 1, 33:34].to_broadcast([128, 33]),
                                          ident[:, :], start=True, stop=True), scd[-1])
                a = V(lambda e: e.tensor_copy(fe[:, 0, :], ps[7][0:33, 0:128]), t2)
                a = V(lambda e: e.tensor_scalar(fe[:, 1, :], wT[0:33, :], -1.0, BIG, ALU.add, ALU.mult), a)
                b = V(lambda e: e.memset(fe[:, 2, :], -BIG))
                a = V(lambda e: e.tensor_tensor_scan(fe[:, 3, :], fe[:, 1, :], fe[:, 0, :], -BIG, ALU.add, ALU.max), a)
                b = V(lambda e: e.tensor_copy(fe[:, 2, 1:128], fe[:, 3, 0:127]), a, b)
                a = V(lambda e: e.tensor_tensor(fe[:, 0, :], fe[:, 0, :], fe[:, 3, :], ALU.subtract), a)
                a = S(lambda e: e.activation(fe[:, 0, :], fe[:, 0, :], ACT.Exp), a)
                a = V(lambda e: e.tensor_tensor(fe[:, 4, :], fe[:, 0, :], ps[6][0:33, 0:128], ALU.mult), a, t1)
                b = V(lambda e: e.tensor_tensor(fe[:, 5, :], fe[:, 2, :], fe[:, 3, :], ALU.subtract), b)
                b = V(lambda e: e.tensor_scalar(fe[:, 5, :], fe[:, 5, :], 0.0, None, ALU.min), b)
                b = S(lambda e: e.activation(fe[:, 5, :], fe[:, 5, :], ACT.Exp), b)
                b = V(lambda e: e.tensor_tensor(fe[:, 5, :], fe[:, 5, :], wT[0:33, :], ALU.mult), b)
                z = V(lambda e: e.memset(fe[:, 7, :], 0.0))
                a = V(lambda e: e.tensor_tensor_scan(fe[:, 6, :], fe[:, 5, :], fe[:, 4, :], 0.0, ALU.mult, ALU.add),
                      a, b)
                a = V(lambda e: e.tensor_copy(fe[:, 7, 1:128], fe[:, 6, 0:127]), a, z)
                t1 = T(lambda e: e.transpose(ps[6][:, 0:33], fe[:, 7, :], ident[0:33, 0:33]), a)
                t2 = T(lambda e: e.transpose(ps[7][:, 0:33], fe[:, 2, :], ident[0:33, 0:33]), a)
                b = V(lambda e: e.tensor_scalar(fs[:, 4:5], pe[:, 0:1], -1.0, BIG, ALU.add, ALU.mult))
                b = V(lambda e: e.scalar_tensor_tensor(out=fs[:, 0:1], in0=ps[7][:, 0:1], scalar=pe[:, 0:1],
                                                       in1=fs[:, 4:5], op0=ALU.mult, op1=ALU.add), b, t2)
                b = V(lambda e: e.tensor_tensor(fs[:, 1:2], fs[:, 0:1], row[:, 33:34], ALU.max), b, g)
                c1 = V(lambda e: e.tensor_tensor(fs[:, 2:3], row[:, 33:34], fs[:, 1:2], ALU.subtract), b)
                c2 = V(lambda e: e.tensor_tensor(fs[:, 3:4], fs[:, 0:1], fs[:, 1:2], ALU.subtract), b)
                c1 = S(lambda e: e.activation(fs[:, 2:4], fs[:, 2:4], ACT.Exp), c1, c2)
                c2 = V(lambda e: e.tensor_tensor(fs[:, 3:4], fs[:, 3:4], pe[:, 0:1], ALU.mult), c1)
                d = V(lambda e: e.tensor_scalar(row2[:, 0:33], row[:, 0:33], fs[:, 2:3], None, ALU.mult), c1)
                d = V(lambda e: e.scalar_tensor_tensor(out=row2[:, 0:33], in0=ps[6][:, 0:33], scalar=fs[:, 3:4],
                                                       in1=row2[:, 0:33], op0=ALU.mult, op1=ALU.add), d, c2, t1)
                d2 = V(lambda e: e.tensor_copy(row2[:, 33:34], fs[:, 1:2]), b)
                fx = scatter(W1, feq[:, 0:1], row2[:, :], "fx", d, d2)
                send(60, 70)
                ng = node_gather(NB, W1, lastq, "ng", fx)
                send(70, J)
                for g in range(NC // GR):
                    c0, c1 = GR * g, GR * g + GR
                    a = V(lambda e, c0=c0, c1=c1: e.tensor_scalar(stb[:, 0, c0:c1], NB[:, c0:c1, 32], 1e-30, None,
                                                                  ALU.max), ng[g])
                    a = V(lambda e, c0=c0, c1=c1: e.reciprocal(stb[:, 0, c0:c1], stb[:, 0, c0:c1]), a)
                    a = V(lambda e, c0=c0, c1=c1: e.tensor_tensor(
                        nd[:, c0:c1, :], NB[:, c0:c1, 0:32], stb[:, 0, c0:c1, None].to_broadcast([128, GR, 32]),
                        ALU.mult), a, ld["ss"])
                    a = V(lambda e, c0=c0, c1=c1: e.tensor_tensor(nd[:, c0:c1, :], nd[:, c0:c1, :], X[:, c0:c1, :],
                                                                  ALU.add), a)
                    layernorm(nd, X, c0, c1, a)

        def layer2():
            with ExitStack() as ph:
                w2s = sb(ph, "w2s", [32, 16, 4, 32])
                rt = sb(ph, "rt", [32, 32])
                bb = sb(ph, "bb", [128, 32])
                XT = sb(ph, "xt2", [32, NC * 128])
                Yb = [sb(ph, f"yb{i}", [128, 2048]) for i in range(2)]
                w2v = w2.rearrange("(b a) i o -> i b a o", a=5)
                for b1 in range(4):
                    for a1 in range(4):
                        for c in range(4):
                            load(w2s[:, 4 * b1 + a1, c, :], w2v[:, b1 + c // 2, a1 + c % 2, :], "w2")
                load(rt[:, :], root2, "w2")
                wl = load(bb[:, :], bias2.rearrange("(o f) -> o f", o=1).to_broadcast([128, 32]), "w2")
                ev, ys, ye = {}, {}, {}
                for c in range(NC):
                    t = T(lambda e, c=c: e.transpose(ps[c % 2][0:32, 0:128], X[:, c, :], ident[:, :]),
                          ev.get(c - 2))
                    ev[c] = V(lambda e, c=c: e.tensor_copy(XT[:, c * 128:(c + 1) * 128], ps[c % 2][0:32, 0:128]), t)
                for c in range(NC):
                    for k in range(4):
                        t = T(lambda e, c=c, k=k: e.matmul(
                            ps[2 + k][:, 0:512], XT[:, c * 128:(c + 1) * 128],
                            w2s[:, 4 * k:4 * k + 4, :, :].rearrange("i a b o -> i (a b o)"), start=True, stop=True),
                            ev[c], wl, ye.get((c - 1, k)))
                        w = V if k % 2 else S
                        ye[(c, k)] = w(lambda e, c=c, k=k: (e.tensor_copy if k % 2 else e.copy)(
                            Yb[c % 2][:, 512 * k:512 * k + 512], ps[2 + k][:, 0:512]), t, ys.get(c - 2))
                    ys[c] = load(Y.rearrange("(p c k) f -> p c (k f)", p=128, c=NC)[:, c, :], Yb[c % 2][:, :],
                                 f"y{c % 2}", ye[(c, 2)], ye[(c, 3)])
                    t = T(lambda e, c=c: e.matmul(ps[6][:, (c % 16) * 32:(c % 16) * 32 + 32],
                                                  XT[:, c * 128:(c + 1) * 128], rt[:, :], start=True, stop=True),
                          ye.get("r"))
                    if c % 16 == 15 or c == NC - 1:
                        n = c % 16 + 1
                        ye["r"] = V(lambda e, c=c, n=n: e.tensor_tensor(
                            RX[:, c - n + 1:c + 1, :], ps[6][:, 0:32 * n].rearrange("p (a b) -> p a b", b=32),
                            bb[:, None, :].to_broadcast([128, n, 32]), ALU.add), t)
                known["y"] = (ys[NC - 1], ys[NC - 2])
                Q.meet(*known["y"])

        def layer2_edges():
            C2 = 28
            with ExitStack() as ph:
                lasts = sb(ph, "lasts", [128, NC], I32)
                feqs = sb(ph, "feqs", [128, 1], I32)
                pes = sb(ph, "pes", [128, 4])
                cTs = sb(ph, "cTs", [64, 128])
                wTs = sb(ph, "wTs", [64, 128])
                ks = sb(ph, "m01s", [128, J])
                t4 = sb(ph, "t4", [128, J, 4], I32)
                kf = sb(ph, "kf2", [128, J])
                q2 = sb(ph, "q2", [128, J])
                pli = sb(ph, "pli2", [128, 1], I32)
                plf = sb(ph, "plf2", [128, 1])
                np2 = node_places(cs, firsts, lasts, None, None)
                z = V(lambda e: e.memset(pli[:, :], -1))
                sent = (known["s40"], known["s41"])
                lt = load(t4[:, :, :], T4.rearrange("(p j) f -> p j f", p=128), "r2", *sent)
                l = load(pli[1:128, :], T4.rearrange("(p j) f -> p j f", p=128)[0:127, J - 1, 0:1], "r3", z)
                a = V(lambda e: e.tensor_copy(kf[:, :], t4[:, :, 0]), lt)
                b = V(lambda e: e.tensor_copy(plf[:, :], pli[:, :]), l)
                c = V(None, a, b)
                mk, sg = segments("sb", kf, plf, c, ks, None, pes, feqs, cTs, wTs, q2, segf)
                Gb = [sb(ph, f"l2g{i}", [128, C2, 4, 32]) for i in range(3)]
                Pb = sb(ph, "l2p", [128, C2, 4, 32])
                wt = sb(ph, "l2w", [128, C2, 4])
                on = sb(ph, "l2n", [128, C2, 2])
                O = [sb(ph, f"l2o{i}", [128, C2, 32]) for i in range(2)]
                CH = chunks(C2)
                N = len(CH)
                prod, scd, stq = [None] * N, [None] * N, [None] * N
                for c, (j0, n) in enumerate(CH):
                    s, s3 = c % 2, c % 3
                    for j in range(n):
                        g = gather(Gb[s3][:, j, :, :].rearrange("p a b -> p (a b)"), Y, t4[:, j0 + j, 1:2],
                                   f"l2g{s3}", prod[c - 3] if c >= 3 else None, lt)
                    fr = t4[:, j0:j0 + n, 2:4].bitcast(F32)
                    a = V(lambda e, fr=fr, n=n: e.tensor_scalar(on[:, 0:n, :], fr, -1.0, 1.0, ALU.mult, ALU.add),
                          lt, prod[c - 1] if c else None)
                    V(lambda e, n=n: e.tensor_tensor(wt[:, 0:n, 0], on[:, 0:n, 0], on[:, 0:n, 1], ALU.mult), a)
                    V(lambda e, fr=fr, n=n: e.tensor_tensor(wt[:, 0:n, 1], fr[:, :, 0], on[:, 0:n, 1], ALU.mult))
                    V(lambda e, fr=fr, n=n: e.tensor_tensor(wt[:, 0:n, 2], on[:, 0:n, 0], fr[:, :, 1], ALU.mult))
                    a = V(lambda e, fr=fr, n=n: e.tensor_tensor(wt[:, 0:n, 3], fr[:, :, 0], fr[:, :, 1], ALU.mult))
                    prod[c] = V(lambda e, n=n, s3=s3: e.tensor_tensor(
                        Pb[:, 0:n, :, :], Gb[s3][:, 0:n, :, :], wt[:, 0:n, :, None].to_broadcast([128, n, 4, 32]),
                        ALU.mult), g, a, scd[c - 1] if c else None)
                    a = V(lambda e, n=n: e.tensor_tensor(Pb[:, 0:n, 0:2, :], Pb[:, 0:n, 0:2, :], Pb[:, 0:n, 2:4, :],
                                                         ALU.add), prod[c])
                    a = V(lambda e, n=n: e.tensor_tensor(Pb[:, 0:n, 0, :], Pb[:, 0:n, 0, :], Pb[:, 0:n, 1, :],
                                                         ALU.add), a)
                    scd[c] = scans(lambda f, s=s, n=n: O[s][:, 0:n, f], ks[:, j0:j0 + n],
                                   lambda f, n=n: Pb[:, 0:n, 0, f],
                                   (lambda f: 0.0) if c == 0 else (lambda f, s=s: O[1 - s][:, C2 - 1, f:f + 1]),
                                   32, ALU.mult, ALU.add, a, mk, stq[c - 2] if c >= 2 else None,
                                   scd[c - 1] if c else None)
                    stq[c] = load(slots(W2, j0, n), O[s][:, 0:n, :], f"l2s{s}", scd[c])
                fx = fixup("f2", O[(N - 1) % 2][:, C2 - 1, :], 32, [(0, 32, False)], W2, feqs, cTs, wTs,
                           (stq[-2], stq[-1], no_edge), V(None, scd[-1], sg))
                ng = node_gather(nd, W2, lasts, "ng", fx, np2)
                a = V(lambda e: e.tensor_scalar(stb[:, 0, :], cs[:, :], 1.0, None, ALU.max))
                rd = V(lambda e: e.reciprocal(stb[:, 0, :], stb[:, 0, :]), a)
                for g in range(NC // GR):
                    c0, c1 = GR * g, GR * g + GR
                    a = V(lambda e, c0=c0, c1=c1: e.tensor_tensor(
                        nd[:, c0:c1, :], nd[:, c0:c1, :], stb[:, 0, c0:c1, None].to_broadcast([128, GR, 32]),
                        ALU.mult), rd, ng[g])
                    a = V(lambda e, c0=c0, c1=c1: e.tensor_tensor(nd[:, c0:c1, :], nd[:, c0:c1, :], RX[:, c0:c1, :],
                                                                  ALU.add), a)
                    a = V(lambda e, c0=c0, c1=c1: e.tensor_tensor(nd[:, c0:c1, :], nd[:, c0:c1, :], X[:, c0:c1, :],
                                                                  ALU.add), a)
                    known[("x3", g)] = layernorm(nd, X, c0, c1, a)

        def layer3():
            with ExitStack() as ph:
                Z = [sb(ph, f"z{i}", [128, GR, 128]) for i in range(2)]
                XC = sb(ph, "xc", [128, NC, 32])
                ZT = [sb(ph, f"zt{i}", [128, GR, 128]) for i in range(2)]
                XT = [sb(ph, f"xt3{i}", [32, GR, 128]) for i in range(2)]
                QN = sb(ph, "qn", [128, NC, 32])
                PN = sb(ph, "pn", [128, NC, 32])
                Gb = [sb(ph, f"l3g{i}", [128, C, 32]) for i in range(2)]
                Ea = [sb(ph, f"l3e{i}", [128, C * 16]) for i in range(2)]
                ET = sb(ph, "l3t", [128, 7, 128])
                Vb = sb(ph, "l3v", [128, C, 32])
                O = [sb(ph, f"l3o{i}", [128, C, 64]) for i in range(2)]
                Zb = O[0][:, 0:NC, :]
                CH = [c for c in chunks(C) if c[0] < J - C] + [(J - 56, 24), (J - 32, 16), (J - 16, 16)]
                N = len(CH)
                bank = {k: None for k in range(8)}
                last = {"xt": {}, "zt": {}, "tq": None, "pn": None}

                lob = sb(ph, "l3lob", [128, J], BF16)
                hib = sb(ph, "l3hib", [128, J], BF16)
                idb = sb(ph, "idb", [128, 128], BF16)
                nio = sb(ph, "nio", [128, 2])
                MB = sb(ph, "mb", [NC, NC, 32], BF16)
                QS = [sb(ph, f"qs{i}", [128, NC * 32], BF16) for i in range(3)]
                LO = [sb(ph, f"lo{i}", [128, KP, 128], BF16) for i in range(2)]
                HI = [sb(ph, f"hi{i}", [NC, KP, 128], BF16) for i in range(2)]
                kf = O[0][:, :, :].rearrange("p a b -> p (a b)")[:, 0:J]
                rk = O[0][:, :, :].rearrange("p a b -> p (a b)")[:, J:2 * J]
                lo = O[1][:, :, :].rearrange("p a b -> p (a b)")[:, 0:J]
                a = V(lambda e: e.tensor_copy(kf, srcs[:, :]))
                with ExitStack() as sp:
                    split = split_key(kf, rk, sb(sp, "l3i", [128, J], I32), a, lo, lob, hib)
                SQ = sb(ph, "sq3", [128, 512])
                PA = sb(ph, "pa", [128, KP, 3, 32])
                idr = V(lambda e: e.tensor_copy(idb[:, :], ident[:, :]))
                nir = V(lambda e: e.tensor_scalar(nio[:, 0:1], iotp[:, :], -1.0, None, ALU.mult))
                nir = V(lambda e: e.memset(nio[:, 1:2], 1.0))
                masked = V(lambda e: e.tensor_scalar(
                    MB[:, :, :], ident[0:NC, 0:NC, None].to_broadcast([NC, NC, 32]), -1.0, BIG, ALU.add, ALU.mult))
                picked, hot, ring = {}, {"pa": split}, [0]

                def parts(ready, read):
                    qf = QN[:, :, :].rearrange("p a b -> p (a b)")
                    r1, r2 = nd2[:, :, :].rearrange("p a b -> p (a b)"), nd[:, :, :].rearrange("p a b -> p (a b)")
                    a = V(lambda e: e.tensor_copy(QS[0][:, :], qf), ready, read)
                    a = V(lambda e: e.tensor_tensor(r1, qf, QS[0][:, :], ALU.subtract), a)
                    a = V(lambda e: e.tensor_copy(QS[1][:, :], r1), a)
                    a = V(lambda e: e.tensor_tensor(r2, r1, QS[1][:, :], ALU.subtract), a)
                    return V(lambda e: e.tensor_copy(QS[2][:, :], r2), a)

                def kp(i):
                    return CH[i % N][1] * KP // C

                def one_hot_steps(i):
                    s, (j0, n), k = i % 2, CH[i % N], kp(i)
                    steps = []
                    for key, P, o in ((lob, 128, LO[s]), (hib, NC, HI[s])):
                        for q in range(0, k, 4):
                            w = min(4, k - q)

                            def step(key=key, P=P, o=o, q=q, w=w):
                                for c in range(w):
                                    j = j0 + n - k + q + c
                                    t = T(lambda e, c=c, j=j: e.matmul(
                                        ps[4][0:P, 128 * c:128 * c + 128], key[:, j:j + 1].to_broadcast([128, P]),
                                        idb[:, :], start=True, stop=True), bank[4], split, idr)
                                a = S(lambda e: e.activation(SQ[0:P, 0:128 * w], ps[4][0:P, 0:128 * w], ACT.Square,
                                                             bias=nio[0:P, 0:1], scale=1.0), t, hot.get("sq"), nir)
                                bank[4] = a
                                hot["sq"] = hot[i] = S(lambda e: e.activation(
                                    o[:, q:q + w, :].rearrange("p a b -> p (a b)"), SQ[0:P, 0:128 * w], ACT.Relu,
                                    bias=nio[0:P, 1:2], scale=-1.0), a, picked.get(i - 2))
                            steps.append(step)
                    return steps

                def pick_rows(i, parted, beside, scans_, free):
                    s, n, k = i % 2, CH[i % N][1], kp(i)
                    for c in range(k):
                        l_, h_ = LO[s][:, c, :], HI[s][:, c, :]
                        for g in range(4):
                            if g < 3:
                                b = ring[0] % 4
                                ring[0] += 1
                                o, r = ps[b][:, 0:512], slice(512 * g, 512 * g + 512)
                            else:
                                b, o, r = 5, ps[5][:, 32 * c:32 * c + 32], slice(1536, 1568)
                            T(lambda e, o=o, r=r, h_=h_: e.matmul(
                                o, h_, MB[:, :, :].rearrange("p a b -> p (a b)")[:, r], start=True, stop=False),
                                hot[i], bank[b], masked, parted)
                            for x in range(3):
                                t = T(lambda e, o=o, r=r, l_=l_, x=x: e.matmul(o, l_, QS[x][:, r], start=False,
                                                                               stop=x == 2))
                            if g < 3:
                                bank[b] = V(lambda e, o=o, c=c, g=g: e.tensor_reduce(
                                    PA[:, c, g, :], o.rearrange("p (h f) -> p f h", f=32), AXX, ALU.max), t,
                                    hot.get("pa"))
                                red = bank[b]
                        for _ in range(-(-len(beside) // (k - c))):
                            beside.pop(0)()
                        for _ in range(-(-len(scans_) // (k - c))):
                            scans_.pop(0)()
                    picked[i] = t
                    a = V(lambda e: e.tensor_tensor(PA[:, 0:k, 0, :], PA[:, 0:k, 0, :], PA[:, 0:k, 1, :], ALU.max), red)
                    b = V(lambda e: e.tensor_tensor(PA[:, 0:k, 2, :], PA[:, 0:k, 2, :],
                                                    ps[5][:, 0:32 * k].rearrange("p (a b) -> p a b", b=32), ALU.max),
                          red, t)
                    bank[5] = b
                    hot["pa"] = V(lambda e: e.tensor_tensor(Gb[s][:, n - k:n, :], PA[:, 0:k, 0, :], PA[:, 0:k, 2, :],
                                                            ALU.max), a, b, free)
                    return hot["pa"]

                def products(l, g, ready):
                    c0, s = GR * g, g % 2
                    for c in range(GR):
                        b = 3 + c // 4
                        t = T(lambda e, c=c, b=b: e.transpose(ps[b][0:32, (c % 4) * 128:(c % 4) * 128 + 128],
                                                              XC[:, c0 + c, :], ident[:, :]), ready, bank[b])
                        if c == 3:
                            t3 = t
                    x1 = S(lambda e: e.copy(XT[s][:, 0:4, :], ps[3][0:32, 0:512].rearrange("p (a b) -> p a b", a=4)),
                           t3, last["xt"].get(s))
                    x2 = S(lambda e: e.copy(XT[s][:, 4:7, :], ps[4][0:32, 0:384].rearrange("p (a b) -> p a b", a=3)),
                           t)
                    bank[3], bank[4] = x1, x2
                    for c in range(GR):
                        t = T(lambda e, c=c: e.matmul(ps[5][:, 64 * c:64 * c + 64], XT[s][:, c, :], BPQ[:, l, :],
                                                      start=True, stop=True), x1 if c < 4 else x2, bank[5])
                    last["xt"][s] = t
                    pv = ps[5][:, 0:64 * GR].rearrange("p (a b) -> p a b", b=64)
                    V(lambda e: e.tensor_copy(PN[:, c0:c0 + GR, :], pv[:, :, 0:32]), t, last["pn"])
                    a = V(lambda e: e.tensor_tensor(QN[:, c0:c0 + GR, :], pv[:, :, 32:64],
                                                    C0[:, l, None, :].to_broadcast([128, GR, 32]), ALU.add), t,
                          last["tq"])
                    bank[5] = last["qn"] = a
                    return load(node_view(TQ)[:, c0:c0 + GR, :], QN[:, c0:c0 + GR, :], "tq", a)

                for g in range(NC // GR):
                    c0 = GR * g
                    a = V(lambda e, c0=c0: e.tensor_copy(XC[:, c0:c0 + GR, :], X[:, c0:c0 + GR, :]), known[("x3", g)])
                    tq = products(0, g, a)
                addd, scd, stq, evr, et = {}, {}, {}, {}, {}
                for step in one_hot_steps(0):
                    step()

                def scan_steps(i, c, j0, n):
                    s, pn = i % 2, CH[c - 1][1]
                    steps = []
                    for base, m, op0, op1, start in ((0, m01, ALU.mult, ALU.add, 0.0),
                                                     (32, mneg, ALU.add, ALU.max, -BIG)):
                        for f in range(32):
                            def step(base=base, m=m, op0=op0, op1=op1, start=start, f=f):
                                ini = start if c == 0 else O[1 - s][:, pn - 1, base + f:base + f + 1]
                                scd[i] = V(lambda e: e.tensor_tensor_scan(
                                    O[s][:, 0:n, base + f], m[:, j0:j0 + n], Vb[:, 0:n, f], ini, op0, op1),
                                    addd[i], stq.get(i - 2), scd.get(i - 1))
                            steps.append(step)

                    def store():
                        stq[i] = load(slots(W3, j0, n), O[s][:, 0:n, :], f"l3s{s}", scd[i])

                    return steps + [store]

                for l in range(5):
                    last["tq"] = tq
                    parted = parts(last["qn"], picked.get(l * N - 1))
                    scans_ = []
                    for c, (j0, n) in enumerate(CH):
                        i = l * N + c
                        s = i % 2
                        for j in range(n - kp(i)):
                            g = gather(Gb[s][:, j, :], TQ, srcs[:, j0 + j:j0 + j + 1], f"l3g{s}", addd.get(i - 2), tq)
                        ld = load(Ea[s][:, 0:16 * n], U["a16"].rearrange("(p j) f -> p (j f)", p=128)[
                            :, j0 * 16:(j0 + n) * 16], f"l3e{s}", et.get(i - 2), in_16)
                        got = pick_rows(i, parted, one_hot_steps(i + 1) if i + 1 < 5 * N else [], scans_,
                                        addd.get(i - 2))
                        for k in range(n // 8):
                            b = 4
                            t = T(lambda e, k=k, s=s, b=b: e.transpose(ps[b][:, 0:128],
                                                                       Ea[s][:, 128 * k:128 * k + 128],
                                                                       ident[:, :]), ld, bank[b])
                            bank[b] = S(lambda e, k=k, b=b: e.copy(ET[:, k, :], ps[b][:, 0:128]), t, evr.get(k))
                            et[i] = t
                            h = 6 + (k // 2) % 2
                            t = T(lambda e, k=k, l=l, h=h: e.matmul(
                                ps[h][:, 256 * (k % 2):256 * (k % 2) + 256], ET[:, k, :],
                                WR[:, l, :, :].rearrange("p a b -> p (a b)"), start=True, stop=True),
                                bank[b], bank[h])
                            evr[k] = t
                            if k % 2 == 1 or k == n // 8 - 1:
                                w = 8 * (k % 2 + 1)
                                a0 = 8 * (k - k % 2)
                                addd[i] = V(lambda e, s=s, h=h, w=w, a0=a0: e.tensor_tensor(
                                    Vb[:, a0:a0 + w, :], Gb[s][:, a0:a0 + w, :],
                                    ps[h][:, 0:32 * w].rearrange("p (a b) -> p a b", b=32), ALU.add), g, got, t,
                                    scd.get(i - 1))
                                bank[h] = addd[i]
                        scans_ = scan_steps(i, c, j0, n)
                    for step in scans_:
                        step()
                    fx = fixup(f"f3{l}", O[s][:, n - 1, :], 64, [(0, 32, False), (32, 64, True)], W3,
                               feq, contT, wT, (stq[i - 1], stq[i], no_edge), scd[i])
                    bank[6] = bank[7] = None
                    ng = node_gather(Zb, W3, lastq, "ng", fx)
                    for g in range(NC // GR):
                        c0, c1, s = GR * g, GR * g + GR, g % 2
                        w = [128, GR, 32]
                        zs, zb = Z[s], Zb
                        free = last["zt"].get(s)
                        V(lambda e, c0=c0, c1=c1, zs=zs: e.tensor_copy(zs[:, :, 0:32], XC[:, c0:c1, :]), free)
                        a = V(lambda e, c0=c0, c1=c1: e.tensor_tensor(
                            nd[:, c0:c1, :], PN[:, c0:c1, :], cnt[:, c0:c1, None].to_broadcast(w), ALU.mult))
                        b = V(lambda e, c0=c0, c1=c1: e.tensor_tensor(
                            nd2[:, c0:c1, :], PN[:, c0:c1, :], Zb[:, c0:c1, 32:64], ALU.add), ng[g])
                        a = V(lambda e, c0=c0, c1=c1, zs=zs: e.tensor_tensor(
                            zs[:, :, 64:96], Zb[:, c0:c1, 0:32], nd[:, c0:c1, :], ALU.add), a)
                        b = V(lambda e, c0=c0, c1=c1, zs=zs: e.tensor_tensor(
                            zs[:, :, 96:128], nd2[:, c0:c1, :], has[:, c0:c1, None].to_broadcast(w), ALU.mult), b)
                        last["pn"] = b
                        a = V(lambda e, c0=c0, c1=c1, zs=zs: e.tensor_tensor(
                            zs[:, :, 32:64], zs[:, :, 64:96], rc[:, c0:c1, None].to_broadcast(w), ALU.mult), a, b)
                        for c in range(GR):
                            k = c // 4
                            t = T(lambda e, c=c, k=k, zs=zs: e.transpose(
                                ps[k][:, (c % 4) * 128:(c % 4) * 128 + 128], zs[:, c, :], ident[:, :]), a, bank[k])
                            if c == 3:
                                t3 = t
                        last["zt"][s] = t
                        x1 = S(lambda e, s=s: e.copy(ZT[s][:, 0:4, :], ps[0][:, 0:512].rearrange(
                            "p (a b) -> p a b", a=4)), t3, last.get(("mm", s)))
                        x2 = S(lambda e, s=s: e.copy(ZT[s][:, 4:7, :], ps[1][:, 0:384].rearrange(
                            "p (a b) -> p a b", a=3)), t)
                        bank[0], bank[1] = x1, x2
                        for c in range(GR):
                            t = T(lambda e, c=c, s=s, l=l: e.matmul(
                                ps[2][:, 32 * c:32 * c + 32], ZT[s][:, c, :], AO[:, l, :], start=True, stop=True),
                                x1 if c < 4 else x2, bank[2])
                        last[("mm", s)] = t
                        a = V(lambda e, l=l, c0=c0, c1=c1: e.tensor_tensor(
                            nd[:, c0:c1, :], ps[2][:, 0:32 * GR].rearrange("p (a b) -> p a b", b=32),
                            CO[:, l, None, :].to_broadcast(w), ALU.add), t)
                        bank[2] = a
                        a = V(lambda e, c0=c0, c1=c1: e.tensor_scalar(XC[:, c0:c1, :], nd[:, c0:c1, :], 0.0, None,
                                                                      ALU.max), a, last["xt"].get("all"))
                        if l < 4:
                            tq = products(l + 1, g, a)
                        else:
                            a = V(lambda e, c0=c0, c1=c1: e.tensor_tensor(
                                nd[:, c0:c1, :], XC[:, c0:c1, :], X[:, c0:c1, :], ALU.add), a)
                            y = layernorm(nd, X, c0, c1, a)
                            ov = out[0:127 * NC, :].rearrange("(p c) f -> p c f", c=NC)
                            load(ov[0:112, c0:c1, :], X[0:112, c0:c1, :], "out", y)
                            o = load(ov[112:127, c0:c1, :], X[112:127, c0:c1, :], "out")
                            n1 = min(c1, NN - 127 * NC)
                            if n1 > c0:
                                o = load(out[127 * NC + c0:127 * NC + n1, :].rearrange("(o c) f -> o c f", o=1),
                                         X[127:128, c0:n1, :], "out")
                    Q.step()
                Q.q["sync"].append((None, (o,), None, None))

        def weights3():
            with ExitStack() as ph:
                PC = sb(ph, "pc", [8, 5, 32])
                EWT = sb(ph, "ewt", [8, 5, 128])
                EB = sb(ph, "ebc", [8, 5])
                PB = sb(ph, "pbc", [128, 5, 32])
                bm = sb(ph, "bm", [128, 8])
                BO = sb(ph, "bo", [32, 5, 4, 32])
                LW = sb(ph, "lw", [32, 5, 32])
                LB_ = sb(ph, "lbb", [128, 5, 32])
                POB = sb(ph, "pobc", [32, 5])
                z1 = V(lambda e: e.memset(BPQ[:, :, :], 0.0))
                z2 = V(lambda e: e.memset(BO[:, :, :, :], 0.0))
                z3 = V(lambda e: e.tensor_reduce(bm[:, :], ident[:, :].rearrange("p (a b) -> p a b", a=8), AXX,
                                                 ALU.add))
                for l in range(5):
                    for t in range(4):
                        r8 = slice(8 * t, 8 * t + 8)
                        load(BPQ[r8, l, 8 * t:8 * t + 8], pW[l, t, 0:8, :], "w3", z1, z2, eng="scalar")
                        load(BPQ[r8, l, 32 + 8 * t:40 + 8 * t], pW[l, t, 8:16, :], "w3", eng="scalar")
                        load(PC[:, l, 8 * t:8 * t + 8], pW[l, t, 16:24, :], "w3", eng="scalar")
                        for i in range(4):
                            load(BO[r8, l, i, 8 * t:8 * t + 8], poW[l, t, 8 * i:8 * i + 8, :].rearrange("k f -> f k"),
                                 "w3", eng="scalar")
                    for j in range(8):
                        load(EWT[:, l, 16 * j:16 * j + 16], eW[l].rearrange("a b -> b a"), "w3", eng="scalar")
                    load(EB[:, l:l + 1], eb[l].rearrange("(a b) -> a b", b=1), "w3", eng="scalar")
                    load(PB[:, l, :], pb[l].rearrange("(o t) f -> o (t f)", o=1).to_broadcast([128, 32]), "w3",
                         eng="scalar")
                    load(LW[:, l, :], lW[l], "w3", eng="scalar")
                    load(LB_[:, l, :], lb[l].rearrange("(o f) -> o f", o=1).to_broadcast([128, 32]), "w3",
                         eng="scalar")
                    wl = load(POB[:, l:l + 1], pob[l].rearrange("t (f o) -> (t f) o", o=1), "w3", eng="scalar")
                pv = [None] * 4
                for l in range(5):
                    t1 = T(lambda e, l=l: e.matmul(ps[0][:, 0:32], EWT[:, l, :], PC[:, l, :], start=True, stop=True),
                           wl, pv[0])
                    pv[0] = V(lambda e, l=l: e.tensor_tensor(
                        WR[:, l, :, :], ps[0][:, None, 0:32].to_broadcast([128, 8, 32]),
                        bm[:, :, None].to_broadcast([128, 8, 32]), ALU.mult), t1, z3)
                    t1 = T(lambda e, l=l: e.matmul(ps[1][:, 0:32], EB[:, l:l + 1].to_broadcast([8, 128]), PC[:, l, :],
                                                   start=True, stop=True), wl, pv[1])
                    pv[1] = V(lambda e, l=l: e.tensor_tensor(C0[:, l, :], ps[1][:, 0:32], PB[:, l, :], ALU.add), t1)
                    t1 = T(lambda e, l=l: e.matmul(ps[2][:, 0:32], BO[:, l, :, :].rearrange("a b c -> a (b c)"),
                                                   LW[:, l, :], start=True, stop=True), wl, pv[2])
                    pv[2] = V(lambda e, l=l: e.tensor_copy(AO[:, l, :], ps[2][:, 0:32]), t1)
                    t1 = T(lambda e, l=l: e.matmul(ps[3][:, 0:32], POB[:, l:l + 1].to_broadcast([32, 128]), LW[:, l, :],
                                                   start=True, stop=True), wl, pv[3])
                    pv[3] = V(lambda e, l=l: e.tensor_tensor(CO[:, l, :], ps[3][:, 0:32], LB_[:, l, :], ALU.add), t1)
                a = V(lambda e: e.tensor_scalar(rc[:, :], cnt[:, :], 1.0, None, ALU.max))
                V(lambda e: e.reciprocal(rc[:, :], rc[:, :]), a)
                V(lambda e: e.tensor_scalar(has[:, :], cnt[:, :], 0.0, None, ALU.is_gt))

        known["X"] = load(X[:, :, :], T0.rearrange("(p c) f -> p c f", p=128), "xin", in_x)
        known["srcs"] = load(srcs[:, :], U["src"][:, 0].rearrange("(p j) -> p j", p=128), "k0", in_src)
        for c in range(2):
            known[("g0", c)] = gather0(c, known["srcs"])
        dst_segments()
        Q.meet(*known["rows"])
        src_work, dst_work = rank_src(), count_dst()
        layer0()
        l0.close()
        layer1()
        Q.meet()
        bgs.close()
        weights3()
        Q.meet()
        layer2()
        early.close()
        Q.meet(known["s40"], known["s41"])
        layer2_edges()
        Q.meet()
        layer3()
        Q.emit()


_INS = ["x", "src", "dst", "edge_attr_16", "edge_attr_2", "edge_attr_32", "L0_gnn_eps", "L1_gnn_beta",
        "L2_gnn_weight", "L2_gnn_root_weight", "L2_gnn_bias", "L3_gnn_edge_W", "L3_gnn_edge_b", "L3_gnn_pre_W",
        "L3_gnn_pre_b", "L3_gnn_post_W", "L3_gnn_post_b", "L3_gnn_lin_W", "L3_gnn_lin_b"]


def kernel(**inputs):
    import numpy as _np
    import concourse.bacc as _bacc
    from concourse.bass_utils import run_bass_kernel_spmd as _run

    nc = _bacc.Bacc("TRN2", target_bir_lowering=False, num_devices=1)
    arrays, args = {}, []
    for name in _INS:
        a = _np.ascontiguousarray(inputs[name])
        arrays[f"in_{name}"] = a
        args.append(nc.dram_tensor(f"in_{name}", a.shape, mybir.dt.from_np(a.dtype), kind="ExternalInput").ap())
    out = nc.dram_tensor("out_0", (NN, 32), F32, kind="ExternalOutput").ap()
    program(nc, *args, out)
    r = _run(nc, [arrays], core_ids=[0])
    return r.results[0]["out_0"]
```
